# Optimizing a Trainium2 kernel written in Bass

```python
import numpy as np
import jax
import jax.numpy as jnp

def _softmax(x, axis=-1):
    return jax.nn.softmax(x, axis=axis)

def _gelu(x):
    return jax.nn.gelu(x, approximate=True)

def _silu(x):
    return jax.nn.silu(x)

def _sigmoid(x):
    return jax.nn.sigmoid(x)

def _layernorm(x, axis=-1, eps=1e-05):
    m = jnp.mean(x, axis=axis, keepdims=True)
    v = jnp.var(x, axis=axis, keepdims=True)
    return (x - m) / jnp.sqrt(v + eps)

def _scatter_add(tgt, idx, src, axis=0):
    return tgt.at[idx].add(src)

def _segment_sum(src, seg, n):
    return jax.ops.segment_sum(src, seg, n)
kernel_name = 'mk_gnn_resnorm_d4_gnn_r8_5fb842'

def setup_inputs(seed: int=0):
    np.random.seed(seed)
    _w = jnp.asarray

    def _rec_inputs():
        import jax
        import jax.numpy as jnp
        _gk = jax.random.key(seed)
        x = -0.0005121 + 1.001 * jax.random.normal(jax.random.fold_in(_gk, 1), (12500, 64), jnp.float32)
        src = jax.random.randint(jax.random.fold_in(_gk, 2), (200000,), 0, 12500, jnp.int32)
        dst = jax.random.randint(jax.random.fold_in(_gk, 3), (200000,), 0, 12500, jnp.int32)
        _o = jnp.argsort(dst, stable=True)
        src = src[_o]
        dst = dst[_o]
        edge_attr_16 = 0.000254156 + 0.999948 * jax.random.normal(jax.random.fold_in(_gk, 12), (200000, 16), jnp.float32)
        edge_attr_2 = -0.000414295 + 0.999828 * jax.random.normal(jax.random.fold_in(_gk, 13), (200000, 2), jnp.float32)
        return (x, src, dst, edge_attr_16, edge_attr_2)
    x, src, dst, edge_attr_16, edge_attr_2 = _rec_inputs()

    def _L0_gnn_setup():
        import jax, jax.numpy as jnp
        import numpy as np
        K = 3
        SLOPE = 0.01
        N_NODES = 6250
        N_EDGES = 100000
        D_IN = 64
        D_OUT = 64
        E_DIM = 2

        def _moments(z_e, Wm_list):
            moms = [z_e]
            mu = z_e.mean(axis=0, keepdims=True)
            for k in range(2, K + 1):
                mk = jnp.mean((z_e - mu) ** k, axis=0)
                mk = jnp.sign(mk) * jnp.abs(mk) ** (1.0 / k)
                moms.append(mk @ Wm_list[k - 2].T)
            return moms
        key = jax.random.key(seed)
        ks = jax.random.split(key, 10)
        s = 0.1
        return {'h': jax.random.normal(ks[0], (N_NODES, D_IN), dtype=jnp.float32), 'e': jax.random.normal(ks[1], (N_EDGES, E_DIM), dtype=jnp.float32), 'src': jax.random.randint(ks[2], (N_EDGES,), 0, N_NODES), 'dst': jax.random.randint(ks[3], (N_EDGES,), 0, N_NODES), 'W_fc': jax.random.normal(ks[4], (D_OUT, D_IN), dtype=jnp.float32) * s, 'W_attn': jax.random.normal(ks[5], (1, 2 * D_OUT * K + E_DIM), dtype=jnp.float32) * s, 'W_edge': jax.random.normal(ks[6], (E_DIM, E_DIM), dtype=jnp.float32) * s, 'W_e2n': jax.random.normal(ks[7], (D_OUT, E_DIM), dtype=jnp.float32) * s, 'W_m1': jax.random.normal(ks[8], (D_OUT, D_OUT), dtype=jnp.float32) * s, 'W_m2': jax.random.normal(ks[9], (D_OUT, D_OUT), dtype=jnp.float32) * s}
    _L0_gnn_all = _L0_gnn_setup()
    _L0_gnn_in = {k: v for k, v in _L0_gnn_all.items() if k in ('W_fc', 'W_attn', 'W_edge', 'W_e2n', 'W_m1', 'W_m2')}
    del _L0_gnn_all

    def _L1_gnn_setup():
        import jax, jax.numpy as jnp
        import numpy as np
        key = jax.random.key(seed)
        k1, k2 = jax.random.split(key)
        N, D, E = (12500, 64, 200000)
        x = jax.random.normal(k1, (N, D), dtype=jnp.float32)
        edge_index = jax.random.randint(k2, (2, E), 0, N, dtype=jnp.int64)
        return {'x': x, 'edge_index': edge_index}
    _L1_gnn_all = _L1_gnn_setup()
    _L1_gnn_in = {k: v for k, v in _L1_gnn_all.items() if k in ()}
    del _L1_gnn_all

    def _L2_gnn_setup():
        import jax, jax.numpy as jnp
        import numpy as np
        N, E, D, ED = (6250, 100000, 64, 16)
        H1 = 2 * D + ED

        def _forward(x, edge_weights, W_att1, b_att1, W_att2, b_att2, W_lin, b_lin, W_ih, b_ih, W_hh, b_hh, edge_idx):
            num_nodes = x.shape[0]
            src = edge_idx[0]
            dst = edge_idx[1]
            lin_x = x @ W_lin.T + b_lin
            feat = jnp.concatenate([x[src], edge_weights, x[dst]], axis=1)
            h = jax.nn.relu(feat @ W_att1.T + b_att1)
            scores = (h @ W_att2.T + b_att2)[:, 0]
            m = jax.ops.segment_max(scores, src, num_segments=num_nodes)
            e = jnp.exp(scores - m[src])
            denom = jax.ops.segment_sum(e, src, num_segments=num_nodes)
            alpha = e / denom[src]
            msg = jax.ops.segment_sum(alpha[:, None] * lin_x[dst], src, num_segments=num_nodes)
            gi = x @ W_ih.T + b_ih
            gh = msg @ W_hh.T + b_hh
            i_r, i_z, i_n = jnp.split(gi, 3, axis=1)
            h_r, h_z, h_n = jnp.split(gh, 3, axis=1)
            r = jax.nn.sigmoid(i_r + h_r)
            z = jax.nn.sigmoid(i_z + h_z)
            n = jnp.tanh(i_n + r * h_n)
            new_h = (1.0 - z) * n + z * msg
            deg = jax.ops.segment_sum(jnp.ones_like(scores), src, num_segments=num_nodes)
            return jnp.where(deg[:, None] > 0, new_h, x)
        key = jax.random.key(seed)
        ks = jax.random.split(key, 16)
        s = 0.05
        inp = {'x': jax.random.normal(ks[0], (N, D), jnp.float32), 'edge_idx': jax.random.randint(ks[1], (2, E), 0, N, jnp.int64), 'edge_weights': jax.random.normal(ks[2], (E, ED), jnp.float32), 'W_att1': jax.random.normal(ks[3], (H1, H1), jnp.float32) * s, 'b_att1': jnp.zeros((H1,), jnp.float32), 'W_att2': jax.random.normal(ks[4], (1, H1), jnp.float32) * s, 'b_att2': jnp.zeros((1,), jnp.float32), 'W_lin': jax.random.normal(ks[5], (D, D), jnp.float32) * s, 'b_lin': jnp.zeros((D,), jnp.float32), 'W_ih': jax.random.normal(ks[6], (3 * D, D), jnp.float32) * s, 'b_ih': jnp.zeros((3 * D,), jnp.float32), 'W_hh': jax.random.normal(ks[7], (3 * D, D), jnp.float32) * s, 'b_hh': jnp.zeros((3 * D,), jnp.float32)}
        return inp
    _L2_gnn_all = _L2_gnn_setup()
    _L2_gnn_in = {k: v for k, v in _L2_gnn_all.items() if k in ('W_att1', 'b_att1', 'W_att2', 'b_att2', 'W_lin', 'b_lin', 'W_ih', 'b_ih', 'W_hh', 'b_hh')}
    del _L2_gnn_all

    def _L3_gnn_setup():
        import jax, jax.numpy as jnp
        import numpy as np
        N_NODES = 12500
        N_EDGES = 200000
        INPUT_DIM = 64
        H_DIM = 1
        key = jax.random.key(seed)
        k_h, k_src, k_dst, k_w, k_b = jax.random.split(key, 5)
        h = jax.random.normal(k_h, (N_NODES, INPUT_DIM), dtype=jnp.float32)
        src = jax.random.randint(k_src, (N_EDGES,), 0, N_NODES, dtype=jnp.int32)
        dst = jax.random.randint(k_dst, (N_EDGES,), 0, N_NODES, dtype=jnp.int32)
        W = jax.random.normal(k_w, (H_DIM, 2 * INPUT_DIM), dtype=jnp.float32) * 0.1
        b = jax.random.normal(k_b, (H_DIM,), dtype=jnp.float32) * 0.1
        return {'h': h, 'src': src, 'dst': dst, 'W': W, 'b': b}
    _L3_gnn_all = _L3_gnn_setup()
    _L3_gnn_in = {k: v for k, v in _L3_gnn_all.items() if k in ('W', 'b')}
    del _L3_gnn_all
    return {'x': x, 'src': src, 'dst': dst, 'edge_attr_16': edge_attr_16, 'edge_attr_2': edge_attr_2, 'L0_gnn_W_fc': _L0_gnn_in['W_fc'], 'L0_gnn_W_attn': _L0_gnn_in['W_attn'], 'L0_gnn_W_edge': _L0_gnn_in['W_edge'], 'L0_gnn_W_e2n': _L0_gnn_in['W_e2n'], 'L0_gnn_W_m1': _L0_gnn_in['W_m1'], 'L0_gnn_W_m2': _L0_gnn_in['W_m2'], 'L2_gnn_W_att1': _L2_gnn_in['W_att1'], 'L2_gnn_b_att1': _L2_gnn_in['b_att1'], 'L2_gnn_W_att2': _L2_gnn_in['W_att2'], 'L2_gnn_b_att2': _L2_gnn_in['b_att2'], 'L2_gnn_W_lin': _L2_gnn_in['W_lin'], 'L2_gnn_b_lin': _L2_gnn_in['b_lin'], 'L2_gnn_W_ih': _L2_gnn_in['W_ih'], 'L2_gnn_b_ih': _L2_gnn_in['b_ih'], 'L2_gnn_W_hh': _L2_gnn_in['W_hh'], 'L2_gnn_b_hh': _L2_gnn_in['b_hh'], 'L3_gnn_W': _L3_gnn_in['W'], 'L3_gnn_b': _L3_gnn_in['b']}

def reference(x, src, dst, edge_attr_16, edge_attr_2, L0_gnn_W_fc, L0_gnn_W_attn, L0_gnn_W_edge, L0_gnn_W_e2n, L0_gnn_W_m1, L0_gnn_W_m2, L2_gnn_W_att1, L2_gnn_b_att1, L2_gnn_W_att2, L2_gnn_b_att2, L2_gnn_W_lin, L2_gnn_b_lin, L2_gnn_W_ih, L2_gnn_b_ih, L2_gnn_W_hh, L2_gnn_b_hh, L3_gnn_W, L3_gnn_b):
    import jax
    import jax.numpy as jnp

    def _L0_gnn_ref(h, e, src, dst, W_fc, W_attn, W_edge, W_e2n, W_m1, W_m2):
        import jax, jax.numpy as jnp
        import numpy as np
        K = 3
        SLOPE = 0.01
        N_NODES = 6250
        N_EDGES = 100000
        D_IN = 64
        D_OUT = 64
        E_DIM = 2

        def _moments(z_e, Wm_list):
            moms = [z_e]
            mu = z_e.mean(axis=0, keepdims=True)
            for k in range(2, K + 1):
                mk = jnp.mean((z_e - mu) ** k, axis=0)
                mk = jnp.sign(mk) * jnp.abs(mk) ** (1.0 / k)
                moms.append(mk @ Wm_list[k - 2].T)
            return moms
        N = h.shape[0]
        D = W_fc.shape[0]
        z = h @ W_fc.T
        z_src = z[src]
        z_dst = z[dst]
        ex = e @ W_edge.T
        wm = [W_m1, W_m2]
        src_m = _moments(z_src, wm)
        dst_m = _moments(z_dst, wm)
        wa = W_attn[0]
        blk = [wa[i * D:(i + 1) * D] for i in range(2 * K)]
        w_e = wa[2 * K * D:]
        a = z_src @ blk[0] + z_dst @ blk[K] + ex @ w_e
        for k in range(1, K):
            a = a + src_m[k] @ blk[k] + dst_m[k] @ blk[K + k]
        att = jnp.where(a > 0, a, SLOPE * a)
        m = jax.ops.segment_max(att, dst, num_segments=N)
        expv = jnp.exp(att - m[dst])
        denom = jax.ops.segment_sum(expv, dst, num_segments=N)
        w = expv / denom[dst]
        ez = ex @ W_e2n.T
        msg = w[:, None] * (z_src + ez)
        return jax.ops.segment_sum(msg, dst, num_segments=N)

    def _L1_gnn_ref(x, edge_index):
        import jax, jax.numpy as jnp
        import numpy as np
        src = edge_index[0]
        dst = edge_index[1]
        msgs = x[src]
        out = jax.ops.segment_sum(msgs, dst, num_segments=x.shape[0])
        return out

    def _L2_gnn_ref(x, edge_idx, edge_weights, W_att1, b_att1, W_att2, b_att2, W_lin, b_lin, W_ih, b_ih, W_hh, b_hh):
        import jax, jax.numpy as jnp
        import numpy as np
        N, E, D, ED = (6250, 100000, 64, 16)
        H1 = 2 * D + ED

        def _forward(x, edge_weights, W_att1, b_att1, W_att2, b_att2, W_lin, b_lin, W_ih, b_ih, W_hh, b_hh, edge_idx):
            num_nodes = x.shape[0]
            src = edge_idx[0]
            dst = edge_idx[1]
            lin_x = x @ W_lin.T + b_lin
            feat = jnp.concatenate([x[src], edge_weights, x[dst]], axis=1)
            h = jax.nn.relu(feat @ W_att1.T + b_att1)
            scores = (h @ W_att2.T + b_att2)[:, 0]
            m = jax.ops.segment_max(scores, src, num_segments=num_nodes)
            e = jnp.exp(scores - m[src])
            denom = jax.ops.segment_sum(e, src, num_segments=num_nodes)
            alpha = e / denom[src]
            msg = jax.ops.segment_sum(alpha[:, None] * lin_x[dst], src, num_segments=num_nodes)
            gi = x @ W_ih.T + b_ih
            gh = msg @ W_hh.T + b_hh
            i_r, i_z, i_n = jnp.split(gi, 3, axis=1)
            h_r, h_z, h_n = jnp.split(gh, 3, axis=1)
            r = jax.nn.sigmoid(i_r + h_r)
            z = jax.nn.sigmoid(i_z + h_z)
            n = jnp.tanh(i_n + r * h_n)
            new_h = (1.0 - z) * n + z * msg
            deg = jax.ops.segment_sum(jnp.ones_like(scores), src, num_segments=num_nodes)
            return jnp.where(deg[:, None] > 0, new_h, x)
        return _forward(x, edge_weights, W_att1, b_att1, W_att2, b_att2, W_lin, b_lin, W_ih, b_ih, W_hh, b_hh, edge_idx)

    def _L3_gnn_ref(h, src, dst, W, b):
        import jax, jax.numpy as jnp
        import numpy as np
        N_NODES = 12500
        N_EDGES = 200000
        INPUT_DIM = 64
        H_DIM = 1
        n = h.shape[0]
        x = jnp.concatenate([h[src], h[dst]], axis=-1)
        e = jax.nn.leaky_relu(x @ W.T + b)
        e_max = jax.ops.segment_max(e, dst, num_segments=n)
        e_exp = jnp.exp(e - e_max[dst])
        e_sum = jax.ops.segment_sum(e_exp, dst, num_segments=n)
        alpha = e_exp / e_sum[dst]
        out = jax.ops.segment_sum(h[src] * alpha, dst, num_segments=n)
        return out
    edge_index = jnp.stack([src, dst])
    x = _layernorm(x + _L0_gnn_ref(x, edge_attr_2, src, dst, L0_gnn_W_fc, L0_gnn_W_attn, L0_gnn_W_edge, L0_gnn_W_e2n, L0_gnn_W_m1, L0_gnn_W_m2), axis=-1)
    x = _layernorm(x + _L1_gnn_ref(x, edge_index), axis=-1)
    x = _layernorm(x + _L2_gnn_ref(x, edge_index, edge_attr_16, L2_gnn_W_att1, L2_gnn_b_att1, L2_gnn_W_att2, L2_gnn_b_att2, L2_gnn_W_lin, L2_gnn_b_lin, L2_gnn_W_ih, L2_gnn_b_ih, L2_gnn_W_hh, L2_gnn_b_hh), axis=-1)
    x = _layernorm(x + _L3_gnn_ref(x, src, dst, L3_gnn_W, L3_gnn_b), axis=-1)
    return x

_drawn_inputs = setup_inputs


def setup_inputs(seed=0):
    import zlib

    import numpy as np

    out = dict(_drawn_inputs(seed))
    spreads = {'L2_gnn_b_att1': (0.0, 0.8),
     'L2_gnn_b_lin': (0.0, 0.1),
     'L2_gnn_b_ih': (0.0, 0.1),
     'L2_gnn_b_hh': (0.0, 0.1)}
    factors = {'edge_attr_16': 8.0,
     'edge_attr_2': 8.0,
     'L0_gnn_W_edge': 8.0,
     'L0_gnn_W_e2n': 8.0,
     'L2_gnn_W_att1': 5.517,
     'L2_gnn_W_att2': 5.901,
     'L2_gnn_W_hh': 3.027}
    for name, (base, spread) in spreads.items():
        noise = np.random.default_rng([zlib.crc32(name.encode()), seed]).standard_normal(out[name].shape)
        drawn = base * np.exp(spread * noise) if base else spread * noise
        out[name] = jnp.asarray(drawn.astype(out[name].dtype))
    for name, factor in factors.items():
        out[name] = (out[name] * factor).astype(out[name].dtype)
    return out
```

```python
from contextlib import ExitStack

import concourse.bass as bass
from concourse import mybir

F32 = mybir.dt.float32
BF16 = mybir.dt.bfloat16
I32 = mybir.dt.int32
ALU = mybir.AluOpType
ACT = mybir.ActivationFunctionType
AX = mybir.AxisListType.X

P = 128
NODES, D = 12500, 64
EDGES = 200000
NB = -(-NODES // P)
LASTN = NODES - (NB - 1) * P
EP, EK = 125, 1600
G = 4
SLOTS = 4
T = -(-((EDGES + NB * (P - 1)) // P) // (G * SLOTS)) * G * SLOTS
STEPS = T // G
SSTEPS = EK // G
TQ = T // 4
EQ = EK // 4
BIG = 2.0 ** 100
CUT = 2.0 ** 120
SLOPE = 0.01
EPS = 1e-5
E2, E16 = 2, 16
REC = {"d": 2 + E2, "s": 2 + E16}
H1 = 2 * D + E16
RW = D + E2 + 1
K3 = 3


def later(s, k):
    return s >= k if isinstance(s, int) else True


class Stage:

    def __init__(self, sem, k, base=0):
        self.sem, self.k, self.base = sem, k, base

    def done(self, s):
        return self.sem, (s + 1) * self.k + self.base

    def part(self, s, j):
        return self.sem, s * self.k + j + self.base


class Chain:

    def __init__(self, sem):
        self.sem, self.n = sem, 0

    def link(self, eng, ins):
        self.n += 1
        ins.then_inc(self.sem, 1)
        eng.wait_ge(self.sem, self.n)


def steps_of(eng, n, unroll, stages):
    lag = max(l for l, _ in stages)

    def one(t, r, j):
        for l, fn in stages:
            s = t - l
            if isinstance(s, int) and not 0 <= s < n:
                continue
            fn(s, r + (j - l) // unroll, (j - l) % unroll)

    first, last = 2 * unroll, n // unroll * unroll
    for t in range(min(first, n)):
        one(t, t // unroll, t % unroll)
    if last > first:
        with eng.Fori(2, last // unroll) as i:
            for j in range(unroll):
                one(i * unroll + j, i, j)
    for t in range(max(last, first), n + lag):
        one(t, t // unroll, t % unroll)


def build(nc, A, out):
    V, PE, AC, GP = nc.vector, nc.tensor, nc.scalar, nc.gpsimd
    with ExitStack() as top:
        def sbt(ctx, name, shape, dt=F32):
            return ctx.enter_context(nc.sbuf_tensor(name, shape, dt))

        def sem(name):
            return top.enter_context(nc.semaphore(name))

        shared = {}

        def again(name, k, n):
            if name not in shared:
                shared[name] = [sem(name), 0]
            st = Stage(shared[name][0], k, shared[name][1])
            shared[name][1] += k * n
            return st

        def dram(name, shape, dt=F32):
            return nc.dram_tensor(name, shape, dt).ap()

        rec = {k: dram(f"rec_{k}", (P * T, REC[k])) for k in "ds"}
        table = [dram(f"table{l}", (NB * P, w)) for l, w in enumerate((D + 1, D, D, D + 1))]
        sums = [dram(f"sums{l}", ((STEPS + 1) * P, G * RW)) for l in range(4)]

        ps = [top.enter_context(nc.psum_tensor(f"bank{i}", [P, 512], F32)) for i in range(8)]

        iota_f = sbt(top, "iota_f", [P, P])
        iota_b = sbt(top, "iota_b", [P, P], BF16)
        iota_col = sbt(top, "iota_col", [P, 1])
        ident = sbt(top, "ident", [P, P])
        ident_b = sbt(top, "ident_b", [P, P], BF16)
        ones = sbt(top, "ones", [P, P])
        X = sbt(top, "X", [P, NB, D])
        carry = {k: sbt(top, f"carry_{k}", [P, T]) for k in "ds"}
        same = sbt(top, "same", [P, T])
        last = {k: sbt(top, f"last_{k}", [1, 2 * NB], I32) for k in "ds"}
        block_of = sbt(top, "block_of", [1, T], I32)
        pick_d = sbt(top, "pick_d", [P, T])
        near = sbt(top, "near", [P, T])
        ew = sbt(top, "ew", [P, E2])
        w_comb = sbt(top, "w_comb", [P, E2, D])

        consts = Chain(sem("consts"))
        loaded = sem("loaded")

        edges = top.enter_context(ExitStack())
        keys = {k: sbt(edges, f"key_{k}", [EP, EK], I32) for k in "ds"}
        hi = {k: sbt(edges, f"hi_{k}", [EP, EK], BF16) for k in "ds"}
        lo = {k: sbt(edges, f"lo_{k}", [EP, EK]) for k in "ds"}
        row = {k: sbt(edges, f"row_{k}", [EP, EK], I32) for k in "ds"}
        other = {"d": "s", "s": "d"}

        scattering = ExitStack()
        stage = {k: sbt(scattering, f"stage_{k}", [EP, SLOTS, G, REC[k]]) for k in "ds"}
        to_row = {k: sbt(scattering, f"to_row_{k}", [EP, SLOTS, G], I32) for k in "ds"}
        ranking = ExitStack()
        e2_all = sbt(ranking, "e2_all", [EP, EK, E2])
        zeros = sbt(ranking, "zeros", [P, 512])
        before = sbt(ranking, "before", [P, P])
        iota_t = sbt(ranking, "iota_t", [P, T])
        pick_s = sbt(ranking, "pick_s", [P, T])
        pick = {"d": pick_d, "s": pick_s}
        pair = sbt(ranking, "pair", [P, T])
        int_a = sbt(ranking, "int_a", [EP, EK], I32)
        mask = sbt(ranking, "mask", [EP, 2, EK], BF16)
        ranks = sbt(ranking, "ranks", [EP, 2, EK])
        mine = sbt(ranking, "mine", [EP, 2, EK])
        count = sbt(ranking, "count", [EP, NB])
        start_row = sbt(ranking, "start_row", [EP, NB])
        tile = sbt(ranking, "tile", [P, 8])
        tile_i = sbt(ranking, "tile_i", [P, 1], I32)
        filling = ExitStack()
        fill = {"d": sbt(filling, "fill_d", [P, T // 4, REC["d"]]), "s": sbt(filling, "fill_s", [P, T // 16, REC["s"]])}
        filled = sem("filled")
        padded = sem("padded")

        def setup_gpsimd(pool):
            link = lambda ins: consts.link(pool, ins)
            for t in (iota_f, iota_b):
                link(GP.iota(t[:], [[1, P]], base=0, channel_multiplier=0, allow_small_or_imprecise_dtypes=True))
            link(GP.iota(iota_col[:], [[0, 1]], base=0, channel_multiplier=1, allow_small_or_imprecise_dtypes=True))
            link(GP.iota(iota_t[:], [[1, T]], base=0, channel_multiplier=0, allow_small_or_imprecise_dtypes=True))
            link(GP.memset(ones[:], 1.0))
            link(GP.memset(zeros[:], 0.0))
            link(GP.affine_select(out=ident[:], in_=ones[:], compare_op=ALU.is_equal, fill=0.0, base=0,
                                  pattern=[[-1, P]], channel_multiplier=1))
            link(GP.affine_select(out=before[:], in_=ones[:], compare_op=ALU.is_gt, fill=0.0, base=0,
                                  pattern=[[1, P]], channel_multiplier=-1))
            link(GP.tensor_copy(ident_b[:], ident[:]))
            for k in "ds":
                link(GP.memset(fill[k][:], 0.0))
                link(GP.memset(fill[k][:, :, 1:2], -1.0))

        N_CONSTS = 13

        def setup_sync(sp):
            for k, a in (("d", "dst"), ("s", "src")):
                sp.dma_start(keys[k][:], A[a].rearrange("(p k) -> p k", p=EP)).then_inc(loaded, 16)
            sp.dma_start(X[:, 0:NB - 1, :],
                         A["x"][0:(NB - 1) * P, :].rearrange("(b p) f -> p b f", p=P)).then_inc(loaded, 16)
            sp.wait_ge(padded, 1)
            sp.dma_start(X[0:LASTN, NB - 1, :], A["x"][(NB - 1) * P:, :]).then_inc(loaded, 16)
            sp.wait_ge(consts.sem, N_CONSTS)
            for k in "ds":
                n = fill[k].shape[1]
                to = rec[k].rearrange("(p c) w -> p c w", p=P)
                for i in range(T // n):
                    sp.dma_start(to[:, i * n:(i + 1) * n, :], fill[k][:]).then_inc(filled, 16)
            for l in range(4):
                sp.dma_start(sums[l][STEPS * P:, :], zeros[:, 0:G * RW]).then_inc(filled, 16)

            sp.wait_ge(filled, 16 * N_FILLED)

        N_FILLED = 4 + 16 + 4

        digits = Chain(sem("digits"))

        def setup_vector(dve):
            V.memset(X[:, NB - 1, :], 0.0).then_inc(padded, 1)
            dve.wait_ge(loaded, 16 * 4)
            for k in "ds":
                digits.link(dve, V.tensor_scalar(int_a[:], keys[k][:], 7, None, ALU.logical_shift_right))
                digits.link(dve, V.tensor_copy(hi[k][:], int_a[:]))
                digits.link(dve, V.tensor_scalar(int_a[:], keys[k][:], P - 1, None, ALU.bitwise_and))
                digits.link(dve, V.tensor_copy(lo[k][:], int_a[:]))

        rk = {k: dict(counted=Stage(sem(f"counted_{k}"), 1), totals=sem(f"totals_{k}"), tiles=sem(f"tiles_{k}"),
                      starts=sem(f"starts_{k}"), picked=sem(f"picked_{k}"), spread=sem(f"spread_{k}"),
                      spread_read=sem(f"spread_read_{k}"), numbers=sem(f"numbers_{k}"),
                      chain=Chain(sem(f"rank_chain_{k}")),
                      ranked=Stage(sem(f"ranked_{k}"), 3), added=Stage(sem(f"added_{k}"), 4)) for k in "ds"}

        def rank_vector(dve, k):
            m = rk[k]
            link = lambda ins: m["chain"].link(dve, ins)
            dve.wait_ge(consts.sem, N_CONSTS)
            def count_block(b, r, u):
                if later(b, 1):
                    dve.wait_ge(*m["counted"].done(b - 1))
                V.tensor_scalar(mask[:, 0, :], hi[k][:], iota_f[0:EP, bass.ds(b, 1)], 0.0, ALU.is_equal, ALU.add,
                                accum_out=count[:, bass.ds(b, 1)]).then_inc(m["counted"].sem, 1)

            steps_of(dve, NB, 2, [(0, count_block)])
            dve.wait_ge(*m["counted"].done(NB - 1))
            c = lambda i: tile[0:NB, i:i + 1]
            dve.wait_ge(m["totals"], 1)
            link(V.tensor_scalar(c(0), ps[0][0:NB, 0:1], float(P - 1), None, ALU.add))
            link(V.tensor_copy(tile_i[0:NB], c(0)))
            link(V.tensor_scalar(tile_i[0:NB], tile_i[0:NB], 7, None, ALU.logical_shift_right))
            V.tensor_copy(c(1), tile_i[0:NB]).then_inc(m["tiles"], 1)
            dve.wait_ge(m["starts"], 1)
            link(V.tensor_copy(c(2), ps[0][0:NB, 1:2]))
            link(V.tensor_tensor(c(3), c(2), c(1), ALU.add))
            link(V.tensor_scalar(c(4), c(2), float(P), None, ALU.mult))
            link(V.tensor_scalar(c(5), c(1), 0.0, None, ALU.is_gt))
            link(V.tensor_scalar(c(6), c(3), -1.0 - T, None, ALU.add))
            link(V.tensor_tensor(c(6), c(6), c(5), ALU.mult))
            link(V.tensor_scalar(c(6), c(6), float(T), None, ALU.add))
            pk, pr = pick[k][0:NB, :], pair[0:NB, :]
            link(V.tensor_scalar(pr, iota_t[0:NB, :], c(2), None, ALU.is_ge))
            link(V.scalar_tensor_tensor(pk, iota_t[0:NB, :], c(3), pr, ALU.is_lt, ALU.mult))
            link(V.memset(pair[0:NB, 0:1], 0.0))
            V.tensor_tensor(pair[0:NB, 1:T], pick[k][0:NB, 1:T], pick[k][0:NB, 0:T - 1],
                            ALU.mult).then_inc(m["picked"], 1)
            dve.wait_ge(m["spread"], 1)
            link(V.tensor_scalar(start_row[:], ps[1][0:EP, 0:NB], -1.0, None, ALU.add))
            link(V.tensor_copy(int_a[0:1, 0:NB], ps[0][0:1, 0:NB]))
            link(V.tensor_scalar(last[k][:, 0:NB], int_a[0:1, 0:NB], 2, None, ALU.logical_shift_right))
            link(V.tensor_scalar(last[k][:, NB:2 * NB], int_a[0:1, 0:NB], G - 1, None, ALU.bitwise_and))
            for i in range(4):
                q = slice(i * TQ, (i + 1) * TQ)
                if k == "d":
                    link(V.tensor_copy(same[:, q], ps[2 + i][:, 0:TQ]))
                V.tensor_scalar(carry[k][:, q], ps[2 + i][:, 0:TQ], -1.0, CUT, ALU.add,
                                ALU.mult).then_inc(m["spread_read"], 1)
            if k == "s":
                dve.wait_ge(m["numbers"], 1)
                for i in range(4):
                    link(V.tensor_copy(block_of[:, i * TQ:(i + 1) * TQ], ps[2 + i][0:1, 0:TQ]))

            ranked, added = m["ranked"], m["added"]

            def rank_block(b, r, u):
                if later(b, 2):
                    dve.wait_ge(*ranked.done(b - 2))
                    dve.wait_ge(*added.done(b - 2))
                V.tensor_scalar(mask[:, u, :], hi[k][:], iota_f[0:EP, bass.ds(b, 1)], None,
                                ALU.is_equal).then_inc(ranked.sem, 1)
                dve.wait_ge(*ranked.part(b, 1))
                V.tensor_tensor_scan(ranks[:, u, :], mask[:, u, :], zero_row, start_row[:, bass.ds(b, 1)], ALU.add,
                                     ALU.add).then_inc(ranked.sem, 1)
                dve.wait_ge(*ranked.part(b, 2))
                V.tensor_tensor(mine[:, u, :], ranks[:, u, :], mask[:, u, :], ALU.mult).then_inc(ranked.sem, 1)

            zero_row = zeros[0:EP, 0:1].to_broadcast([EP, EK])
            steps_of(dve, NB, 2, [(0, rank_block)])
            dve.wait_ge(*added.done(NB - 1))
            for i in range(4):
                link(V.tensor_copy(row[k][:, i * EQ:(i + 1) * EQ], ps[4 + i][0:EP, 0:EQ]))
            link(V.tensor_scalar(int_a[:], row[k][:], P - 1, None, ALU.bitwise_and))
            link(V.tensor_scalar(row[k][:], row[k][:], 7, None, ALU.logical_shift_right))
            link(V.tensor_copy(ranks[:, 0, :], row[k][:]))
            link(V.scalar_tensor_tensor(row[k][:], int_a[:], float(T), ranks[:, 0, :], ALU.mult, ALU.add))

        def rank_tensor(pe, k):
            m = rk[k]
            c = lambda i: tile[0:NB, i:i + 1]
            pe.wait_ge(consts.sem, N_CONSTS)
            pe.wait_ge(*m["counted"].done(NB - 1))
            PE.matmul(ps[0][0:NB, 0:1], count[:], ones[0:EP, 0:1], start=True, stop=True).then_inc(m["totals"], 1)
            pe.wait_ge(m["tiles"], 1)
            PE.matmul(ps[0][0:NB, 1:2], before[0:NB, 0:NB], c(1), start=True, stop=True).then_inc(m["starts"], 1)
            pe.wait_ge(m["picked"], 1)
            PE.matmul(ps[1][0:EP, 0:NB], c(4).to_broadcast([NB, EP]), ident[0:NB, 0:NB], start=True, stop=False)
            PE.matmul(ps[1][0:EP, 0:NB], before[0:EP, 0:EP], count[:], start=False, stop=True)
            PE.matmul(ps[0][0:1, 0:NB], c(6), ident[0:NB, 0:NB], start=True, stop=True)
            for i in range(4):
                mm = PE.matmul(ps[2 + i][:, 0:TQ], ones[0:NB, :], pair[0:NB, i * TQ:(i + 1) * TQ], start=True,
                               stop=True)
            mm.then_inc(m["spread"], 1)
            pe.wait_ge(m["spread_read"], 4)
            if k == "s":
                for i in range(4):
                    mm = PE.matmul(ps[2 + i][0:1, 0:TQ], iota_col[0:NB, :], pick_s[0:NB, i * TQ:(i + 1) * TQ],
                                   start=True, stop=True)
                mm.then_inc(m["numbers"], 1)
            def add_block(b, r, u):
                pe.wait_ge(*m["ranked"].done(b))
                for i in range(4):
                    PE.matmul(ps[4 + i][0:EP, 0:EQ], ident[0:EP, 0:EP], mine[:, u, i * EQ:(i + 1) * EQ],
                              start=isinstance(b, int) and b == 0, stop=True,
                              skip_group_check=True).then_inc(m["added"].sem, 1)

            steps_of(pe, NB, 2, [(0, add_block)])

        with nc.Block() as block:
            @block.gpsimd
            def _(pool):
                setup_gpsimd(pool)

            @block.sync
            def _(sp):
                setup_sync(sp)

            @block.vector
            def _(dve):
                setup_vector(dve)
                rank_vector(dve, "d")

            @block.tensor
            def _(pe):
                rank_tensor(pe, "d")

        filling.close()

        e2_loaded = sem("e2_loaded")
        e16_loaded = [sem(f"e16_loaded{u}") for u in range(SLOTS)]
        staged = {k: Stage(sem(f"staged_{k}"), 4 if k == "d" else 3) for k in "ds"}
        taken = {k: [sem(f"taken_{k}{u}") for u in range(SLOTS)] for k in "ds"}
        scatters = sem("scatters")

        def stage_scalar(act, k):
            if k == "d":
                act.wait_ge(e2_loaded, 16)
            inc = staged[k].sem

            def one(s, r, u):
                if later(s, SLOTS):
                    act.wait_ge(taken[k][u], r * 16 * G)
                cols = bass.ds(s * G, G)
                AC.copy(stage[k][:, u, :, 0:1].bitcast(I32), keys[other[k]][:, cols, None]).then_inc(inc, 1)
                AC.copy(stage[k][:, u, :, 1:2], lo[k][:, cols, None]).then_inc(inc, 1)
                AC.copy(to_row[k][:, u, :], row[k][:, cols]).then_inc(inc, 1)
                if k == "d":
                    AC.copy(stage[k][:, u, :, 2:4], e2_all[:, cols, :]).then_inc(inc, 1)

            steps_of(act, SSTEPS, SLOTS, [(0, one)])

        def stage_sync(sp, k):
            if k == "d":
                sp.dma_start(e2_all[:], A["e2"].rearrange("(p k) e -> p k e", p=EP)).then_inc(e2_loaded, 16)
                return
            e16 = A["e16"].rearrange("(p k) e -> p k e", p=EP)

            def one(s, r, u):
                if later(s, SLOTS):
                    sp.wait_ge(taken[k][u], r * 16 * G)
                sp.dma_start(stage[k][:, u, :, 2:], e16[:, bass.ds(s * G, G), :]).then_inc(e16_loaded[u], 16)

            steps_of(sp, SSTEPS, SLOTS, [(0, one)])

        def scatter_gpsimd(pool, k):
            def one(s, r, u):
                pool.wait_ge(*staged[k].done(s))
                if k == "s":
                    pool.wait_ge(e16_loaded[u], (r + 1) * 16)
                pool.sem_inc(scatters, 1)
                for g in range(G):
                    GP.indirect_dma_start(rec[k], bass.IndirectOffsetOnAxis(to_row[k][:, u, g:g + 1], 0),
                                          stage[k][:, u, g, :], None).then_inc(taken[k][u], 16)

            steps_of(pool, SSTEPS, SLOTS, [(0, one)])
            for u in range(SLOTS):
                pool.wait_ge(taken[k][u], SSTEPS // SLOTS * 16 * G)

        with nc.Block() as block:
            @block.gpsimd
            def _(pool):
                scatter_gpsimd(pool, "d")

            @block.scalar
            def _(act):
                stage_scalar(act, "d")

            @block.sync
            def _(sp):
                stage_sync(sp, "d")

            @block.vector
            def _(dve):
                rank_vector(dve, "s")

            @block.tensor
            def _(pe):
                rank_tensor(pe, "s")
        ranking.close()

        nodes0 = ExitStack()
        Z = sbt(nodes0, "Z", [P, NB, D + 1])
        far = sbt(nodes0, "far", [P, NB])
        dev = sbt(nodes0, "dev", [P, NB, D])
        power = sbt(nodes0, "power", [P, NB, D])
        degree = {k: sbt(nodes0, f"degree_{k}", [P, NB]) for k in "ds"}
        hot_lo = sbt(nodes0, "hot_lo", [EP, 2, G, P], BF16)
        hot_hi = sbt(nodes0, "hot_hi", [EP, 2, G, NB], BF16)
        x_block = sbt(nodes0, "x_block", [P, 2, P])
        x_turned = sbt(nodes0, "x_turned", [D, 2, P])
        w_fc = sbt(nodes0, "w_fc", [D, D])
        w_z = sbt(nodes0, "w_z", [D, D + 2])
        attn_cols = sbt(nodes0, "attn_cols", [D, 2 * K3])
        attn_edge = sbt(nodes0, "attn_edge", [E2, 1])
        w_edge = sbt(nodes0, "w_edge", [E2, E2])
        w_e2n_t = sbt(nodes0, "w_e2n_t", [E2, D])
        w_m = sbt(nodes0, "w_m", [D, 2, D])
        moment_w = sbt(nodes0, "moment_w", [P, 4, D])
        part = sbt(nodes0, "part", [P, D])
        mean = sbt(nodes0, "mean", [P, D])
        moment = sbt(nodes0, "moment", [P, 4, D])
        root = sbt(nodes0, "root", [P, 4, D])
        sign = sbt(nodes0, "sign", [P, 2, D])
        shift = sbt(nodes0, "shift", [P, 1])
        far_t = sbt(nodes0, "far_t", [NB, P])
        w_loaded = sem("w_loaded")
        weights = dict(made=sem("weights_made"), read=sem("weights_read"))
        hist = {k: dict(hot=Stage(sem(f"hot_{k}"), 2 * G), summed=Stage(sem(f"hist_{k}"), 1)) for k in "ds"}
        zs = dict(block=Stage(sem("z_block"), 1), turned=Stage(sem("z_turned"), 1), kept=Stage(sem("z_kept"), 1),
                  made=Stage(sem("z_made"), 1), out=Stage(sem("z_out"), 2))
        nodes0_chain = Chain(sem("nodes0_chain"))
        partial = Stage(sem("partial"), 1)
        spread_sum = Stage(sem("spread_sum"), 1)
        moments_in, roots_out = sem("moments_in"), sem("roots_out")
        far_turned, far_kept, near_made = sem("far_turned"), sem("far_kept"), sem("near_made")
        z_stored = sem("z_stored")

        def weights_sync(sp):
            for to, a in ((w_fc[:], "w_fc"), (w_z[:, 0:D], "w_fc_t"), (attn_cols[:], "attn_cols"),
                          (attn_edge[:], "attn_edge"), (w_edge[:], "w_edge"), (w_e2n_t[:], "w_e2n_t"),
                          (w_m[:, 0, :], "w_m1"), (w_m[:, 1, :], "w_m2")):
                sp.dma_start(to, A[a]).then_inc(w_loaded, 16)

        N_WEIGHTS = 8
        MOMENT_OF = ((0, 1), (0, 4), (1, 2), (1, 5))

        def weights_tensor(pe):
            pe.wait_ge(w_loaded, 16 * N_WEIGHTS)
            w = ps[7]
            PE.matmul(w[0:D, 0:2], w_fc[:], attn_cols[:, 0:K3 + 1:K3], start=True, stop=True)
            PE.matmul(w[:, 2:4], attn_edge[:].to_broadcast([E2, P]), w_edge[:], start=True, stop=True)
            for j in range(E2):
                PE.matmul(w[:, 4 + j * D:4 + (j + 1) * D], w_edge[:, j:j + 1].to_broadcast([E2, P]), w_e2n_t[:],
                          start=True, stop=True)
            for i, (m, v) in enumerate(MOMENT_OF):
                o = 4 + (E2 + i) * D
                mm = PE.matmul(w[:, o:o + D], attn_cols[:, v:v + 1].to_broadcast([D, P]), w_m[:, m, :], start=True,
                               stop=True)
            mm.then_inc(weights["made"], 1)

        def weights_vector(dve):
            link = lambda ins: nodes0_chain.link(dve, ins)
            dve.wait_ge(weights["made"], 1)
            w = ps[7]
            link(V.tensor_copy(w_z[:, D:D + 2], w[0:D, 0:2]))
            link(V.tensor_copy(ew[:], w[:, 2:4]))
            link(V.tensor_copy(w_comb[:].rearrange("p e f -> p (e f)"), w[:, 4:4 + E2 * D]))
            V.tensor_copy(moment_w[:].rearrange("p m f -> p (m f)"),
                          w[:, 4 + E2 * D:4 + (E2 + 4) * D]).then_inc(weights["read"], 1)

        def hist_vector(dve, k):
            hot, summed = hist[k]["hot"], hist[k]["summed"]

            def one(s, r, u):
                if later(s, 2):
                    dve.wait_ge(*summed.done(s - 2))
                    dve.wait_ge(*hot.done(s - 2))
                for g in range(G):
                    V.tensor_scalar(hot_lo[:, u, g, :], iota_b[0:EP, :], lo[k][:, bass.ds(s * G + g, 1)], None,
                                    ALU.is_equal).then_inc(hot.sem, 1)
                    V.tensor_scalar(hot_hi[:, u, g, :], iota_b[0:EP, 0:NB], hi[k][:, bass.ds(s * G + g, 1)], None,
                                    ALU.is_equal).then_inc(hot.sem, 1)

            steps_of(dve, SSTEPS, 2, [(0, one)])
            dve.wait_ge(*summed.done(SSTEPS - 1))
            nodes0_chain.link(dve, V.tensor_copy(degree[k][:], ps["ds".index(k)][:, 0:NB]))

        def hist_tensor(pe, k):
            hot, summed = hist[k]["hot"], hist[k]["summed"]

            def one(s, r, u):
                pe.wait_ge(*hot.done(s))
                for g in range(G):
                    mm = PE.matmul(ps["ds".index(k)][:, 0:NB], hot_lo[:, u, g, :], hot_hi[:, u, g, :],
                                   start=isinstance(s, int) and s == 0 and g == 0, stop=True, skip_group_check=True)
                mm.then_inc(summed.sem, 1)

            steps_of(pe, SSTEPS, 2, [(0, one)])

        def z_vector(dve):
            nodes0_chain.link(dve, V.memset(x_block[:], 0.0))

            def block(b, r, u):
                if later(b, 2):
                    dve.wait_ge(*zs["turned"].done(b - 2))
                    dve.wait_ge(*zs["block"].done(b - 2))
                V.tensor_copy(x_block[:, u, None, 0:D], X[:, bass.ds(b, 1), :]).then_inc(zs["block"].sem, 1)

            def keep(b, r, u):
                dve.wait_ge(*zs["turned"].done(b))
                if later(b, 2):
                    dve.wait_ge(*zs["made"].done(b - 2))
                V.tensor_copy(x_turned[:, u, :], ps[2 + u][0:D, 0:P]).then_inc(zs["kept"].sem, 1)

            def project(b, r, u):
                dve.wait_ge(*zs["made"].done(b))
                V.tensor_copy(Z[:, bass.ds(b, 1), :], ps[4 + u][:, None, 0:D + 1]).then_inc(zs["out"].sem, 1)
                V.tensor_copy(far[:, bass.ds(b, 1)], ps[4 + u][:, D + 1:D + 2]).then_inc(zs["out"].sem, 1)

            steps_of(dve, NB, 2, [(0, block), (1, keep), (2, project)])
            dve.wait_ge(*zs["out"].done(NB - 1))

        def z_tensor(pe):
            pe.wait_ge(weights["read"], 1)

            def turn(b, r, u):
                pe.wait_ge(*zs["block"].done(b))
                if later(b, 2):
                    pe.wait_ge(*zs["kept"].done(b - 2))
                PE.transpose(ps[2 + u][:, 0:P], x_block[:, u, :], ident[:]).then_inc(zs["turned"].sem, 1)

            def project(b, r, u):
                pe.wait_ge(*zs["kept"].done(b))
                if later(b, 2):
                    pe.wait_ge(*zs["out"].done(b - 2))
                PE.matmul(ps[4 + u][:, 0:D + 2], x_turned[:, u, :], w_z[:], start=True,
                          stop=True).then_inc(zs["made"].sem, 1)

            steps_of(pe, NB, 2, [(0, turn), (1, project)])

        def over_nodes(a):
            return a[:].rearrange("p b f -> p f b")

        def wide(a):
            return a[:, :, None].to_broadcast([P, NB, D])

        def moments_vector(dve):
            link = lambda ins: nodes0_chain.link(dve, ins)
            n = 0

            def total(src, to, n):
                V.tensor_reduce(part[:], over_nodes(src), AX, ALU.add).then_inc(partial.sem, 1)
                dve.wait_ge(*spread_sum.done(n))
                link(V.tensor_scalar(to, ps[6][:, 0:D], 1.0 / EDGES, None, ALU.mult))

            for i, k in enumerate("sd"):
                link(V.tensor_tensor(power[:], Z[:, :, 0:D], wide(degree[k]), ALU.mult))
                total(power, mean[:], n)
                n += 1
                link(V.tensor_tensor(dev[:], Z[:, :, 0:D], mean[:, None, :].to_broadcast([P, NB, D]), ALU.subtract))
                link(V.tensor_tensor(power[:], dev[:], dev[:], ALU.mult))
                link(V.tensor_tensor(power[:], power[:], wide(degree[k]), ALU.mult))
                total(power, moment[:, i, :], n)
                n += 1
                link(V.tensor_tensor(power[:], power[:], dev[:], ALU.mult))
                total(power, moment[:, 2 + i, :], n)
                n += 1
            link(V.tensor_scalar(sign[:], moment[:, 2:4, :], 0.0, None, ALU.is_ge))
            link(V.tensor_scalar(sign[:], sign[:], 2.0, -1.0, ALU.mult, ALU.add))
            link(V.tensor_tensor(moment[:, 2:4, :], moment[:, 2:4, :], sign[:], ALU.mult))
            V.tensor_scalar(moment[:], moment[:], 1e-37, None, ALU.max).then_inc(moments_in, 1)
            dve.wait_ge(roots_out, 3)
            link(V.tensor_tensor(root[:, 2:4, :], root[:, 2:4, :], sign[:], ALU.mult))
            link(V.tensor_tensor(root[:], root[:], moment_w[:], ALU.mult))
            link(V.tensor_reduce(shift[:], root[:].rearrange("p m f -> p (m f)"), AX, ALU.add))
            V.tensor_scalar(far[:], far[:], shift[:, 0:1], None, ALU.add).then_inc(far_turned, 1)
            near_vector(dve, nodes0_chain, far_turned, far_t, far_kept, near_made)

        def near_vector(dve, chain, turned, t, kept, made):
            dve.wait_ge(turned, 2)
            V.tensor_copy(t[:], ps[6][0:NB, 0:P]).then_inc(kept, 1)
            dve.wait_ge(made, 1)
            for i in range(4):
                chain.link(dve, V.tensor_copy(near[:, i * TQ:(i + 1) * TQ], ps[i][:, 0:TQ]))

        def near_tensor(pe, col, turned, t, kept, made):
            pe.wait_ge(turned, 1)
            PE.transpose(ps[6][0:NB, 0:P], col[:], ident[:]).then_inc(turned, 1)
            pe.wait_ge(kept, 1)
            for i in range(4):
                mm = PE.matmul(ps[i][:, 0:TQ], t[:], pick_d[0:NB, i * TQ:(i + 1) * TQ], start=True, stop=True)
            mm.then_inc(made, 1)

        def moments_tensor(pe):
            for n in range(6):
                pe.wait_ge(*partial.done(n))
                PE.matmul(ps[6][:, 0:D], ones[:], part[:], start=True, stop=True).then_inc(spread_sum.sem, 1)
            near_tensor(pe, far, far_turned, far_t, far_kept, near_made)

        def moments_scalar(act):
            act.wait_ge(moments_in, 1)
            AC.sqrt(root[:, 0:2, :], moment[:, 0:2, :]).then_inc(roots_out, 1)
            AC.activation(root[:, 2:4, :], moment[:, 2:4, :], ACT.Ln).then_inc(roots_out, 1)
            act.wait_ge(roots_out, 2)
            AC.activation(root[:, 2:4, :], root[:, 2:4, :], ACT.Exp, scale=1.0 / 3.0).then_inc(roots_out, 1)

        with nc.Block() as block:
            @block.gpsimd
            def _(pool):
                scatter_gpsimd(pool, "s")

            @block.sync
            def _(sp):
                weights_sync(sp)
                stage_sync(sp, "s")
                sp.wait_ge(*zs["out"].done(NB - 1))
                sp.dma_start(table[0].rearrange("(b p) w -> p b w", p=P), Z[:]).then_inc(z_stored, 16)
                sp.wait_ge(z_stored, 16)

            @block.scalar
            def _(act):
                stage_scalar(act, "s")
                moments_scalar(act)

            @block.vector
            def _(dve):
                weights_vector(dve)
                z_vector(dve)
                hist_vector(dve, "d")
                hist_vector(dve, "s")
                moments_vector(dve)

            @block.tensor
            def _(pe):
                weights_tensor(pe)
                z_tensor(pe)
                hist_tensor(pe, "d")
                hist_tensor(pe, "s")
                moments_tensor(pe)

        nodes0.close()
        scattering.close()
        edges.close()

        def edge_layer(l, k, kind, A_all=None, w_in=None, w_out=None, b_out=None):
            soft, gated = kind != "sum", kind == "gated"
            W = {"moments": RW, "sum": D, "gated": D + 1, "plain": D + 1}[kind]
            TW = D + 1 if kind in ("moments", "plain") else D
            VW = D + E16
            look = 1 if gated else 2
            lag = 2 if gated else 1
            NTB = 3 if gated else 2
            name = lambda s: f"l{l}_{s}"
            with ExitStack() as ctx:
                buf = lambda n, shape, dt=F32: sbt(ctx, name(n), shape, dt)
                slab = buf("slab", [P, SLOTS, G, REC[k]])
                rows = buf("rows", [P, SLOTS, G, VW])
                hot = buf("hot", [P, SLOTS, G, P])
                kept = buf("kept", [P, SLOTS, G * W])
                if soft:
                    far_off = buf("far_off", [P, SLOTS, G, P], BF16)
                    turned = buf("turned", [P, SLOTS, G, P])
                    score = buf("score", [P, SLOTS, G])
                    at_node = buf("at_node", [P, SLOTS, G, 2])
                    top_ = buf("top", [P, 2, G])
                    best = buf("best", [P, SLOTS, G + 1])
                    gaps = buf("gaps", [P, SLOTS, 2, G])
                    factor = buf("factor", [P, SLOTS, 2, G])
                    arg = buf("arg", [P, SLOTS, 3, G])
                    message = buf("message", [P, SLOTS, G, W])
                    scaled = buf("scaled", [P, 2, G * W])
                if gated:
                    feat = buf("feat", [P, 2, G, P])
                    junk = buf("junk", [P, 2, H1])
                st = lambda n, c: again(n, c, STEPS)
                ring = lambda n, c: [again(f"{n}{u}", c, STEPS // SLOTS) for u in range(SLOTS)]
                slab_in, rows_in, saved = ring("slab_in", 16), ring("rows_in", 16 * G), ring("saved", 16)
                S = dict(hot=st("hot", 2 * G if soft else G), agg=st("agg", 1), kept=st("kept", G))
                cleared = Chain(sem(name("cleared")))
                gathers = again("gathers", 1, STEPS).sem
                if soft:
                    S.update(off=st("off", 1), turned=st("turned", 1), score=st("score", {"moments": 2, "plain": 1,
                             "gated": G + 1}[kind]), spread=st("spread", 1), top=st("top", 1),
                             node=st("node", 1 if gated else 4), gaps=st("gaps", 5), carried=st("carried", 1),
                             factor=st("factor", 1), arg=st("arg", 2 if gated else 4), weight=st("weight", 1),
                             message=st("message", 2 if kind == "moments" else 1), scaled=st("scaled", 1))
                if gated:
                    S.update(edge=st("edge", 1), flipped=st("flipped", 1), feat=st("feat", 1), hidden=st("hidden", 1))
                done = lambda n, s: S[n].done(s)
                sum_bank = lambda u: ps[6 + u % 2]
                LK = G * W
                read_last = "message" if soft else "kept"

                def gather_gpsimd(pool):
                    def one(s, r, u):
                        if later(s, SLOTS):
                            pool.wait_ge(*done(read_last, s - SLOTS))
                        pool.wait_ge(*slab_in[u].done(r))
                        pool.sem_inc(gathers, 1)
                        for g in range(G):
                            GP.indirect_dma_start(rows[:, u, g, 0:TW], None, table[l],
                                                  bass.IndirectOffsetOnAxis(slab[:, u, g, 0:1].bitcast(I32), 0)
                                                  ).then_inc(rows_in[u].sem, 16)

                    steps_of(pool, STEPS, UN, [(0, lambda s, r, u: one(s, s_div(s, r, u), u % SLOTS))])

                UN = SLOTS * NTB if gated else SLOTS

                def s_div(s, r, u):
                    return r * (UN // SLOTS) + u // SLOTS

                def records_sync(sp):
                    src = rec[k].rearrange("(p t) w -> p t w", p=P)

                    def load(s, r, u):
                        if later(s, SLOTS):
                            sp.wait_ge(*done(read_last, s - SLOTS))
                        sp.dma_start(slab[:, u % SLOTS, :, :],
                                     src[:, bass.ds(s * G, G), :]).then_inc(slab_in[u % SLOTS].sem, 16)

                    def save(s, r, u):
                        sp.wait_ge(*done("kept", s))
                        sp.dma_start(sums[l][bass.ds(s * P, P), 0:G * W],
                                     kept[:, u % SLOTS, :]).then_inc(saved[u % SLOTS].sem, 16)

                    steps_of(sp, STEPS, UN, [(0, load), (lag + 1, save)])
                    for u in range(SLOTS):
                        sp.wait_ge(*saved[u].done(STEPS // SLOTS - 1))

                def edge_vector(dve):
                    cleared.link(dve, V.memset(kept[:, SLOTS - 1, :], 0.0))
                    if soft:
                        cleared.link(dve, V.memset(best[:, SLOTS - 1, :], -CUT))
                    prev = lambda u: (u - 1) % SLOTS

                    def make_hot(s, r, u):
                        u4 = u % SLOTS
                        if later(s, 1):
                            dve.wait_ge(*(done("message", s - lag - 1) if soft and later(s, lag + 1)
                                          else done("hot", s - 1)))
                        if later(s, SLOTS):
                            dve.wait_ge(*done("agg", s - SLOTS))
                        dve.wait_ge(*slab_in[u4].done(s_div(s, r, u)))
                        for g in range(G):
                            V.tensor_scalar(hot[:, u4, g, :], iota_f[:], slab[:, u4, g, 1:2], None,
                                            ALU.is_equal).then_inc(S["hot"].sem, 1)
                            if soft:
                                V.tensor_scalar(far_off[:, u4, g, :], iota_b[:], slab[:, u4, g, 1:2], -BIG,
                                                ALU.not_equal, ALU.mult).then_inc(S["hot"].sem, 1)

                    def make_score(s, r, u):
                        u4 = u % SLOTS
                        inc = S["score"].sem
                        sc, sl, rw = score[:, u4, :, None], slab[:, u4], rows[:, u4]
                        if gated:
                            dve.wait_ge(*done("hidden", s))
                            for g in range(G):
                                if g >= 2:
                                    dve.wait_ge(*S["score"].part(s, g - 1))
                                V.scalar_tensor_tensor(junk[:, g % 2, :], ps[4 + g // 2][:, g % 2 * 256:g % 2 * 256 + H1],
                                                       0.0, w_out[:], ALU.max, ALU.mult,
                                                       accum_out=score[:, u4, g:g + 1]).then_inc(inc, 1)
                            dve.wait_ge(*S["score"].part(s, G))
                            V.tensor_scalar(score[:, u4, :], score[:, u4, :], b_out[:, 0:1], None,
                                            ALU.add).then_inc(inc, 1)
                            return
                        dve.wait_ge(*rows_in[u4].done(s_div(s, r, u)))
                        if kind == "plain":
                            V.tensor_copy(sc, rw[:, :, D:D + 1]).then_inc(inc, 1)
                            return
                        V.scalar_tensor_tensor(sc, sl[:, :, 2:3], ew[:, 0:1], rw[:, :, D:D + 1], ALU.mult,
                                               ALU.add).then_inc(inc, 1)
                        dve.wait_ge(*S["score"].part(s, 1))
                        V.scalar_tensor_tensor(sc, sl[:, :, 3:4], ew[:, 1:2], sc, ALU.mult, ALU.add).then_inc(inc, 1)

                    def make_shift(s, r, u):
                        u4 = u % SLOTS
                        node, cols = S["node"], bass.ds(s * G, G)
                        dve.wait_ge(*done("spread", s))
                        bank = ps[u % NTB][:].rearrange("p (g e) -> p g e", g=G)
                        mine = at_node[:, u4, :, 1:2]
                        if gated:
                            V.tensor_reduce(mine, bank, AX, ALU.max).then_inc(S["top"].sem, 1)
                            dve.wait_ge(*done("top", s))
                            V.tensor_copy(top_[:, 0, :], at_node[:, u4, :, 1]).then_inc(node.sem, 1)
                        else:
                            V.tensor_reduce(top_[:, 0, :, None], bank, AX, ALU.max).then_inc(S["top"].sem, 1)
                            V.tensor_copy(at_node[:, u4, :, 0:1], near[:, cols, None]).then_inc(node.sem, 1)
                            dve.wait_ge(*done("top", s))
                            V.tensor_tensor(top_[:, 1, :], top_[:, 0, :], near[:, cols], ALU.add).then_inc(node.sem, 1)
                            dve.wait_ge(*node.part(s, 2))
                            V.scalar_tensor_tensor(mine, top_[:, 1, :, None], SLOPE, top_[:, 1, :, None], ALU.mult,
                                                   ALU.max).then_inc(node.sem, 1)
                            dve.wait_ge(*node.part(s, 3))
                            V.tensor_copy(top_[:, 0, :], at_node[:, u4, :, 1]).then_inc(node.sem, 1)
                        gp = S["gaps"]
                        V.tensor_copy(best[:, u4, 0:1], best[:, prev(u4), G:G + 1]).then_inc(gp.sem, 1)
                        dve.wait_ge(*done("node", s))
                        V.tensor_tensor_scan(best[:, u4, 1:G + 1], carry[k][:, cols], top_[:, 0, :],
                                             best[:, prev(u4), G:G + 1], ALU.add, ALU.max).then_inc(gp.sem, 1)
                        dve.wait_ge(*gp.part(s, 2))
                        V.tensor_tensor(gaps[:, u4, 0, :], best[:, u4, 0:G], carry[k][:, cols],
                                        ALU.add).then_inc(gp.sem, 1)
                        V.tensor_tensor(gaps[:, u4, 1, :], top_[:, 0, :], best[:, u4, 1:G + 1],
                                        ALU.subtract).then_inc(gp.sem, 1)
                        dve.wait_ge(*gp.part(s, 3))
                        V.tensor_tensor(gaps[:, u4, 0, :], gaps[:, u4, 0, :], best[:, u4, 1:G + 1],
                                        ALU.subtract).then_inc(gp.sem, 1)

                    def make_arg(s, r, u):
                        u4 = u % SLOTS
                        a, ar = S["arg"], arg[:, u4]
                        dve.wait_ge(*done("carried", s))
                        carried = sum_bank(u)[:, LK:LK + G * look].rearrange("p (g c) -> p g c", c=look)
                        if gated:
                            V.tensor_tensor(ar[:, 1, :, None], score[:, u4, :, None], carried,
                                            ALU.subtract).then_inc(a.sem, 1)
                        else:
                            V.tensor_tensor(ar[:, 0, :, None], score[:, u4, :, None], carried[:, :, 0:1],
                                            ALU.add).then_inc(a.sem, 1)
                            dve.wait_ge(*a.part(s, 1))
                            V.scalar_tensor_tensor(ar[:, 1, :], ar[:, 0, :], SLOPE, ar[:, 0, :], ALU.mult,
                                                   ALU.max).then_inc(a.sem, 1)
                            dve.wait_ge(*a.part(s, 2))
                            V.tensor_tensor(ar[:, 1, :, None], ar[:, 1, :, None], carried[:, :, 1:2],
                                            ALU.subtract).then_inc(a.sem, 1)
                        dve.wait_ge(*a.part(s, a.k - 1))
                        V.tensor_scalar(ar[:, 2, :], ar[:, 1, :], 1.0, None, ALU.min).then_inc(a.sem, 1)

                    def make_message(s, r, u):
                        u4 = u % SLOTS
                        dve.wait_ge(*done("weight", s))
                        w = message[:, u4, :, W - 1:W]
                        V.tensor_tensor(message[:, u4, :, 0:D], rows[:, u4, :, 0:D], w.to_broadcast([P, G, D]),
                                        ALU.mult).then_inc(S["message"].sem, 1)
                        if kind == "moments":
                            V.tensor_tensor(message[:, u4, :, D:D + E2], slab[:, u4, :, 2:4],
                                            w.to_broadcast([P, G, E2]), ALU.mult).then_inc(S["message"].sem, 1)

                    def scale_sums(s, r, u):
                        u4 = u % SLOTS
                        dve.wait_ge(*done("agg", s))
                        dve.wait_ge(*done("factor", s))
                        V.tensor_tensor(scaled[:, u % 2, :].rearrange("p (g w) -> p g w", g=G),
                                        sum_bank(u)[:, 0:G * W].rearrange("p (g w) -> p g w", g=G),
                                        factor[:, u4, 1, :, None].to_broadcast([P, G, W]),
                                        ALU.mult).then_inc(S["scaled"].sem, 1)

                    def add_sums(s, r, u):
                        u4 = u % SLOTS
                        kp = S["kept"]
                        if later(s, SLOTS):
                            dve.wait_ge(*saved[u4].done(s_div(s, r, u) - 1))
                        if soft:
                            dve.wait_ge(*done("scaled", s))
                        else:
                            dve.wait_ge(*done("agg", s))
                        for g in range(G):
                            if later(s * G + g if isinstance(s, int) else s, 1):
                                dve.wait_ge(*kp.part(s, g))
                            old = kept[:, u4, (g - 1) * W:g * W] if g else kept[:, prev(u4), (G - 1) * W:]
                            by = factor[:, u4, 0, g:g + 1] if soft else same[:, bass.ds(s * G + g, 1)]
                            new = scaled[:, u % 2, g * W:(g + 1) * W] if soft else sum_bank(u)[:, g * W:(g + 1) * W]
                            V.scalar_tensor_tensor(kept[:, u4, g * W:(g + 1) * W], old, by, new, ALU.mult,
                                                   ALU.add).then_inc(kp.sem, 1)

                    if soft:
                        steps_of(dve, STEPS, UN, [(lag, make_score), (0, make_hot), (lag, make_shift),
                                                  (lag + 1, scale_sums), (lag, make_arg), (lag + 1, add_sums),
                                                  (lag, make_message)])
                    else:
                        steps_of(dve, STEPS, UN, [(0, make_hot), (lag, add_sums)])

                def edge_tensor(pe):
                    def node_mask(s, r, u):
                        u4 = u % SLOTS
                        pe.wait_ge(*done("hot", s))
                        if later(s, NTB):
                            pe.wait_ge(*done("top", s - NTB))
                        for g in range(G):
                            mm = PE.matmul(ps[u % NTB][:, g * P:(g + 1) * P], far_off[:, u4, g, :], ident_b[:],
                                           start=g == 0, stop=False, skip_group_check=True)
                        mm.then_inc(S["off"].sem, 1)

                    def add_scores(s, r, u):
                        u4 = u % SLOTS
                        pe.wait_ge(*done("score", s))
                        pe.wait_ge(*done("turned", s))
                        for g in range(G):
                            mm = PE.matmul(ps[u % NTB][:, g * P:(g + 1) * P],
                                           score[:, u4, g:g + 1].to_broadcast([P, P]), ident[:],
                                           start=False, stop=True, skip_group_check=True)
                        mm.then_inc(S["spread"].sem, 1)

                    def carry_over(s, r, u):
                        u4 = u % SLOTS
                        pe.wait_ge(*done("node", s))
                        if later(s, 2):
                            pe.wait_ge(*done("arg", s - 2))
                            pe.wait_ge(*done("scaled", s - 2))
                        for g in range(G):
                            mm = PE.matmul(sum_bank(u)[:, LK + g * look:LK + (g + 1) * look], turned[:, u4, g, :],
                                           at_node[:, u4, g, 2 - look:2], start=True, stop=True,
                                           skip_group_check=True)
                        mm.then_inc(S["carried"].sem, 1)

                    def sum_edges(s, r, u):
                        u4 = u % SLOTS
                        if soft:
                            pe.wait_ge(*done("message", s))
                        else:
                            pe.wait_ge(*done("hot", s))
                            pe.wait_ge(*rows_in[u4].done(s_div(s, r, u)))
                            if later(s, 2):
                                pe.wait_ge(*done("kept", s - 2))
                        for g in range(G):
                            rhs = message[:, u4, g, :] if soft else rows[:, u4, g, 0:D]
                            mm = PE.matmul(sum_bank(u)[:, g * W:(g + 1) * W], hot[:, u4, g, :], rhs, start=True,
                                           stop=True, skip_group_check=True)
                        mm.then_inc(S["agg"].sem, 1)

                    def flip(s, r, u):
                        u4 = u % SLOTS
                        pe.wait_ge(*done("edge", s))
                        pe.wait_ge(*rows_in[u4].done(s_div(s, r, u)))
                        if later(s, 1):
                            pe.wait_ge(*done("feat", s - 1))
                        for g in range(G):
                            mm = PE.matmul(ps[3][0:VW, g * P:(g + 1) * P], rows[:, u4, g, :], ident[:], start=True,
                                           stop=True, is_transpose=True, skip_group_check=True)
                        mm.then_inc(S["flipped"].sem, 1)

                    def hidden(s, r, u):
                        u4 = u % SLOTS
                        near_block = [pe.value_load(block_of[0:1, bass.ds(s * G + g, 1)], min_val=0, max_val=NB - 1)
                                      for g in range(G)]
                        pe.wait_ge(*done("feat", s))
                        pe.wait_ge(*done("turned", s))
                        if later(s, 1):
                            pe.wait_ge(*done("score", s - 1))
                        for g in range(G):
                            o = ps[4 + g // 2][:, g % 2 * 256:g % 2 * 256 + H1]
                            PE.matmul(o, feat[0:VW, u % 2, g, :], w_in[0:VW, :], start=True, stop=False,
                                      skip_group_check=True)
                            mm = PE.matmul(o, turned[:, u4, g, :], A_all[:, bass.ds(near_block[g], 1), :],
                                           start=False, stop=True, skip_group_check=True)
                        mm.then_inc(S["hidden"].sem, 1)

                    if gated:
                        steps_of(pe, STEPS, UN, [(lag, add_scores), (0, node_mask), (1, flip), (lag, carry_over),
                                                 (1, hidden), (lag, sum_edges)])
                    elif soft:
                        steps_of(pe, STEPS, UN, [(lag, add_scores), (0, node_mask), (lag, carry_over),
                                                 (lag, sum_edges)])
                    else:
                        steps_of(pe, STEPS, UN, [(0, sum_edges)])

                def edge_scalar(act):
                    def turn(s, r, u):
                        u4 = u % SLOTS
                        act.wait_ge(*done("off", s))
                        if later(s, SLOTS):
                            act.wait_ge(*done("carried", s - SLOTS))
                        AC.activation(turned[:, u4].rearrange("p g e -> p (g e)"), ps[u % NTB][:], ACT.Relu,
                                      bias=1.0, scale=1.0 / BIG).then_inc(S["turned"].sem, 1)

                    def edge_features(s, r, u):
                        u4 = u % SLOTS
                        act.wait_ge(*slab_in[u4].done(s_div(s, r, u)))
                        if later(s, SLOTS):
                            act.wait_ge(*done("message", s - SLOTS))
                        AC.copy(rows[:, u4, :, D:VW], slab[:, u4, :, 2:]).then_inc(S["edge"].sem, 1)

                    def keep_flipped(s, r, u):
                        act.wait_ge(*done("flipped", s))
                        if later(s, 2):
                            act.wait_ge(*done("hidden", s - 2))
                        AC.copy(feat[0:VW, u % 2].rearrange("p g e -> p (g e)"),
                                ps[3][0:VW, :]).then_inc(S["feat"].sem, 1)

                    def factors(s, r, u):
                        u4 = u % SLOTS
                        act.wait_ge(*done("gaps", s))
                        if later(s, SLOTS):
                            act.wait_ge(*done("kept", s - SLOTS))
                        AC.activation(factor[:, u4], gaps[:, u4], ACT.Exp).then_inc(S["factor"].sem, 1)

                    def weight(s, r, u):
                        u4 = u % SLOTS
                        act.wait_ge(*done("arg", s))
                        if later(s, SLOTS):
                            act.wait_ge(*done("agg", s - SLOTS))
                        AC.activation(message[:, u4, :, W - 1:W], arg[:, u4, 2, :, None],
                                      ACT.Exp).then_inc(S["weight"].sem, 1)

                    if gated:
                        steps_of(act, STEPS, UN, [(0, edge_features), (0, turn), (1, keep_flipped), (lag, factors),
                                                  (lag, weight)])
                    else:
                        steps_of(act, STEPS, UN, [(0, turn), (lag, factors), (lag, weight)])

                with nc.Block() as block:
                    @block.gpsimd
                    def _(pool):
                        gather_gpsimd(pool)

                    @block.sync
                    def _(sp):
                        records_sync(sp)

                    @block.vector
                    def _(dve):
                        edge_vector(dve)

                    @block.tensor
                    def _(pe):
                        edge_tensor(pe)

                    if soft:
                        @block.scalar
                        def _(act):
                            edge_scalar(act)

        fetched = [[sem(f"fetched{l}_{h}") for h in range(2)] for l in range(4)]

        def fetch(eng, l, k, half, to, W):
            src = sums[l].rearrange("(s p) w -> s p w", p=P)[:, :, 0:G * W].rearrange("s p (g w) -> s p g w", g=G)
            lo_b, hi_b = half * (NB // 2), (half + 1) * (NB // 2)
            with eng.Fori(lo_b, hi_b) as b:
                step = eng.value_load(last[k][0:1, bass.ds(b, 1)], min_val=0, max_val=STEPS)
                place = eng.value_load(last[k][0:1, bass.ds(b + NB, 1)], min_val=0, max_val=G - 1)
                eng.dma_start(to[:, bass.ds(b, 1), :],
                              src[bass.ds(step, 1), :, bass.ds(place, 1), :].rearrange("s p g w -> (s p) g w")
                              ).then_inc(fetched[l][half], 16)
            eng.wait_ge(fetched[l][half], 16 * (NB // 2))

        eps = sbt(top, "eps", [P, 1])
        norm = [dict(var=sem(f"norm_var{l}"), root=sem(f"norm_root{l}")) for l in range(4)]

        def norm_vector(dve, chain, l, Y, ctx_tiles):
            sq, mean_n, var_n = ctx_tiles
            link = lambda ins: chain.link(dve, ins)
            link(V.memset(eps[:], EPS))
            link(V.tensor_reduce(mean_n[:], Y[:], AX, ALU.add))
            link(V.tensor_scalar(mean_n[:], mean_n[:], 1.0 / D, None, ALU.mult))
            link(V.tensor_tensor(Y[:], Y[:], wide(mean_n), ALU.subtract))
            link(V.tensor_tensor(sq[:], Y[:], Y[:], ALU.mult))
            V.tensor_reduce(var_n[:], sq[:], AX, ALU.add).then_inc(norm[l]["var"], 1)
            dve.wait_ge(norm[l]["root"], 1)
            link(V.reciprocal(var_n[:], var_n[:]))
            V.tensor_tensor(X[:], Y[:], wide(var_n), ALU.mult).then_inc(xs_ready[l], 1)
            dve.wait_ge(xs_ready[l], 1)

        def norm_scalar(act, l, var_n):
            act.wait_ge(norm[l]["var"], 1)
            AC.activation(var_n[:], var_n[:], ACT.Sqrt, bias=eps[:], scale=1.0 / D).then_inc(norm[l]["root"], 1)

        def divide(dve, chain, all_, W, over):
            link = lambda ins: chain.link(dve, ins)
            w = all_[:, :, W - 1]
            link(V.tensor_scalar(over[:], w, 0.0, None, ALU.is_equal))
            link(V.tensor_tensor(over[:], over[:], w, ALU.add))
            link(V.reciprocal(over[:], over[:]))

        def node_tiles(ctx, l, W):
            return dict(got=sbt(ctx, f"got{l}", [P, NB, W]), Y=sbt(ctx, f"Y{l}", [P, NB, D]),
                        sq=sbt(ctx, f"sq{l}", [P, NB, D]), mean=sbt(ctx, f"mean{l}", [P, NB]),
                        var=sbt(ctx, f"var{l}", [P, NB]), over=sbt(ctx, f"over{l}", [P, NB]))

        stored = sem("stored")
        xs_ready = [sem(f"x_ready{l}") for l in range(4)]
        row3 = lambda a: a[:, None, :].to_broadcast([P, NB, D])

        edge_layer(0, "d", "moments")
        with ExitStack() as ctx:
            t = node_tiles(ctx, 0, RW)
            chain = Chain(sem("node_chain0"))
            with nc.Block() as block:
                @block.sync
                def _(sp):
                    fetch(sp, 0, "d", 0, t["got"], RW)
                    sp.wait_ge(xs_ready[0], 1)
                    sp.dma_start(table[1].rearrange("(b p) w -> p b w", p=P), X[:]).then_inc(stored, 16)
                    sp.wait_ge(stored, 16)

                @block.scalar
                def _(act):
                    fetch(act, 0, "d", 1, t["got"], RW)
                    norm_scalar(act, 0, t["var"])

                @block.vector
                def _(dve):
                    link = lambda ins: chain.link(dve, ins)
                    for h in range(2):
                        dve.wait_ge(fetched[0][h], 16 * (NB // 2))
                    divide(dve, chain, t["got"], RW, t["over"])
                    link(V.tensor_tensor(t["Y"][:], t["got"][:, :, D:D + 1].to_broadcast([P, NB, D]),
                                         row3(w_comb[:, 0, :]), ALU.mult))
                    link(V.tensor_tensor(t["sq"][:], t["got"][:, :, D + 1:D + 2].to_broadcast([P, NB, D]),
                                         row3(w_comb[:, 1, :]), ALU.mult))
                    link(V.tensor_tensor(t["Y"][:], t["Y"][:], t["sq"][:], ALU.add))
                    link(V.tensor_tensor(t["Y"][:], t["Y"][:], t["got"][:, :, 0:D], ALU.add))
                    link(V.tensor_tensor(t["Y"][:], t["Y"][:], wide(t["over"]), ALU.mult))
                    link(V.tensor_tensor(t["Y"][:], t["Y"][:], X[:], ALU.add))
                    norm_vector(dve, chain, 0, t["Y"], (t["sq"], t["mean"], t["var"]))

        edge_layer(1, "d", "sum")
        with ExitStack() as ctx:
            t = node_tiles(ctx, 1, D)
            chain = Chain(sem("node_chain1"))
            with nc.Block() as block:
                @block.sync
                def _(sp):
                    fetch(sp, 1, "d", 0, t["got"], D)
                    sp.wait_ge(xs_ready[1], 1)
                    sp.dma_start(table[2].rearrange("(b p) w -> p b w", p=P), X[:]).then_inc(stored, 16)
                    sp.wait_ge(stored, 32)

                @block.scalar
                def _(act):
                    fetch(act, 1, "d", 1, t["got"], D)
                    norm_scalar(act, 1, t["var"])

                @block.vector
                def _(dve):
                    for h in range(2):
                        dve.wait_ge(fetched[1][h], 16 * (NB // 2))
                    chain.link(dve, V.tensor_tensor(t["Y"][:], t["got"][:], X[:], ALU.add))
                    norm_vector(dve, chain, 1, t["Y"], (t["sq"], t["mean"], t["var"]))

        gated = ExitStack()
        w_in = sbt(gated, "w_in", [D + E16, H1])
        w_near = sbt(gated, "w_near", [D + 1, H1])
        w_out = sbt(gated, "w_out", [P, H1])
        b_out = sbt(gated, "b_out", [P, 1])
        A_all = sbt(gated, "A_all", [P, NB, H1])
        w2_loaded = sem("w2_loaded")

        pre = dict(block=Stage(sem("a_block"), 1), turned=Stage(sem("a_turned"), 1), kept=Stage(sem("a_kept"), 1),
                   made=Stage(sem("a_made"), 1), out=Stage(sem("a_out"), 1), init=sem("a_init"))
        with ExitStack() as ctx:
            b_block = sbt(ctx, "b_block", [P, 2, P])
            b_turned = sbt(ctx, "b_turned", [P, 2, P])
            with nc.Block() as block:
                @block.sync
                def _(sp):
                    for to, a in ((w_in[0:D, :], A["w_att1_t"][D + E16:, :]), (w_in[D:, :], A["w_att1_t"][D:D + E16, :]),
                                  (w_near[0:D, :], A["w_att1_t"][0:D, :]), (w_near[D:, :], A["b_att1"][None, :]),
                                  (w_out[:], A["w_att2"].to_broadcast([P, H1])),
                                  (b_out[:], A["b_att2"][None, :].to_broadcast([P, 1]))):
                        sp.dma_start(to, a).then_inc(w2_loaded, 16)
                    sp.wait_ge(w2_loaded, 16 * 6)

                @block.vector
                def _(dve):
                    V.memset(b_block[:], 0.0).then_inc(pre["init"], 1)
                    dve.wait_ge(pre["init"], 1)
                    V.memset(b_block[:, :, D:D + 1], 1.0).then_inc(pre["init"], 1)
                    dve.wait_ge(pre["init"], 2)

                    def stage_block(b, r, u):
                        if later(b, 2):
                            dve.wait_ge(*pre["turned"].done(b - 2))
                            dve.wait_ge(*pre["block"].done(b - 2))
                        V.tensor_copy(b_block[:, u, None, 0:D], X[:, bass.ds(b, 1), :]).then_inc(pre["block"].sem, 1)

                    def keep(b, r, u):
                        dve.wait_ge(*pre["turned"].done(b))
                        if later(b, 2):
                            dve.wait_ge(*pre["made"].done(b - 2))
                        V.tensor_copy(b_turned[:, u, :], ps[2 + u][:, 0:P]).then_inc(pre["kept"].sem, 1)

                    def drain(b, r, u):
                        dve.wait_ge(*pre["made"].done(b))
                        V.tensor_copy(A_all[:, bass.ds(b, 1), :], ps[4 + u][:, None, 0:H1]).then_inc(pre["out"].sem, 1)

                    steps_of(dve, NB, 2, [(0, stage_block), (1, keep), (2, drain)])

                @block.tensor
                def _(pe):
                    pe.wait_ge(w2_loaded, 16 * 6)
                    pe.wait_ge(pre["init"], 2)

                    def turn(b, r, u):
                        pe.wait_ge(*pre["block"].done(b))
                        if later(b, 2):
                            pe.wait_ge(*pre["kept"].done(b - 2))
                        PE.transpose(ps[2 + u][:, 0:P], b_block[:, u, :], ident[:]).then_inc(pre["turned"].sem, 1)

                    def project(b, r, u):
                        pe.wait_ge(*pre["kept"].done(b))
                        if later(b, 2):
                            pe.wait_ge(*pre["out"].done(b - 2))
                        PE.matmul(ps[4 + u][:, 0:H1], b_turned[0:D + 1, u, :], w_near[:], start=True,
                                  stop=True).then_inc(pre["made"].sem, 1)

                    steps_of(pe, NB, 2, [(0, turn), (1, project)])

        edge_layer(2, "s", "gated", A_all, w_in, w_out, b_out)
        gated.close()

        GW = 5 * D
        gate = ExitStack()
        gru = dict(block=Stage(sem("g_block"), 2), turned=Stage(sem("g_turned"), 2), kept=Stage(sem("g_kept"), 1),
                   made=Stage(sem("g_made"), 1), sig=Stage(sem("g_sig"), 1), part=Stage(sem("g_part"), 4),
                   reset=Stage(sem("g_reset"), 2), tanh=Stage(sem("g_tanh"), 1), new=Stage(sem("g_new"), 3),
                   init=sem("g_init"), w=sem("g_w"), made_w=sem("g_made_w"), scaled=sem("g_scaled"))
        with ExitStack() as ctx:
            t = node_tiles(ctx, 2, D + 1)
            w_x = sbt(ctx, "w_x", [D + 1, 3 * D])
            w_msg = sbt(ctx, "w_msg", [D + 1, 4 * D])
            w_hh_t = sbt(ctx, "w_hh_t", [D, 3 * D])
            w_lin = sbt(ctx, "w_lin", [D, D + 1])
            two = sbt(ctx, "two", [P, 2, 2, P])
            two_t = sbt(ctx, "two_t", [P, 2, 2, P])
            gates = sbt(ctx, "gates", [P, 2, 2 * D])
            gates1 = sbt(ctx, "gates1", [P, 2, 2 * D])
            cand = sbt(ctx, "cand", [P, 2, D])
            own = sbt(ctx, "own", [P, NB], I32)
            chain = Chain(sem("node_chain2"))
            with nc.Block() as block:
                @block.sync
                def _(sp):
                    for to, a in ((w_x[0:D, :], A["w_ih_t"]), (w_x[D:, :], A["b_ih"][None, :]),
                                  (w_hh_t[:], A["w_hh_t"]), (w_lin[:, 0:D], A["w_lin"]),
                                  (w_lin[:, D:], A["b_lin"][:, None]), (w_msg[0:D, 3 * D:], A["w_lin_t"]),
                                  (w_msg[D:, 3 * D:], A["b_lin"][None, :]), (cand[D:D + 1, :, :],
                                  A["b_hh"][0:2 * D].rearrange("(o a f) -> o a f", o=1, a=2)),
                                  (gates[D:D + 1, 0, 0:D], A["b_hh"][None, 2 * D:])):
                        sp.dma_start(to, a).then_inc(gru["w"], 16)
                    fetch(sp, 2, "s", 0, t["got"], D + 1)

                @block.scalar
                def _(act):
                    fetch(act, 2, "s", 1, t["got"], D + 1)

                    def sigmoid_half(b, r, u):
                        act.wait_ge(*gru["made"].done(b))
                        if later(b, 2):
                            act.wait_ge(*gru["new"].done(b - 2))
                        AC.activation(gates[:, u, :], ps[4 + u][:, 0:2 * D], ACT.Tanh,
                                      scale=0.5).then_inc(gru["sig"].sem, 1)

                    def candidate(b, r, u):
                        act.wait_ge(*gru["reset"].done(b))
                        AC.activation(cand[:, u, :], cand[:, u, :], ACT.Tanh).then_inc(gru["tanh"].sem, 1)

                    steps_of(act, NB, 2, [(1, candidate), (0, sigmoid_half)])
                    norm_scalar(act, 2, t["var"])

                @block.tensor
                def _(pe):
                    pe.wait_ge(gru["w"], 16 * 9)
                    PE.matmul(ps[0][0:D + 1, 0:3 * D], w_lin[:], w_hh_t[:], start=True,
                              stop=True).then_inc(gru["made_w"], 1)
                    pe.wait_ge(gru["init"], 2)

                    def turn(b, r, u):
                        pe.wait_ge(*gru["block"].done(b))
                        if later(b, 2):
                            pe.wait_ge(*gru["kept"].done(b - 2))
                        for i in range(2):
                            PE.transpose(ps[2 + u][:, i * P:(i + 1) * P], two[:, u, i, :],
                                         ident[:]).then_inc(gru["turned"].sem, 1)

                    def project(b, r, u):
                        pe.wait_ge(*gru["kept"].done(b))
                        if later(b, 2):
                            pe.wait_ge(*gru["new"].done(b - 2))
                        o = ps[4 + u]
                        PE.matmul(o[:, 0:3 * D], two_t[0:D + 1, u, 0, :], w_x[:], start=True, stop=False,
                                  skip_group_check=True)
                        PE.matmul(o[:, 0:2 * D], two_t[0:D + 1, u, 1, :], w_msg[:, 0:2 * D], start=False, stop=True,
                                  skip_group_check=True)
                        PE.matmul(o[:, 3 * D:GW], two_t[0:D + 1, u, 1, :], w_msg[:, 2 * D:], start=False, stop=True,
                                  skip_group_check=True).then_inc(gru["made"].sem, 1)

                    steps_of(pe, NB, 2, [(0, turn), (1, project)])

                @block.vector
                def _(dve):
                    link = lambda ins: chain.link(dve, ins)
                    dve.wait_ge(gru["made_w"], 1)
                    link(V.tensor_copy(w_msg[0:D, 0:3 * D], ps[0][0:D, 0:3 * D]))
                    link(V.tensor_tensor(w_msg[D:D + 1, 0:2 * D], ps[0][D:D + 1, 0:2 * D],
                                         cand[D:D + 1, :, :].rearrange("p a f -> p (a f)"), ALU.add))
                    link(V.tensor_tensor(w_msg[D:D + 1, 2 * D:3 * D], ps[0][D:D + 1, 2 * D:3 * D],
                                         gates[D:D + 1, 0, 0:D], ALU.add))
                    link(V.memset(two[:], 0.0))
                    V.memset(two[:, :, :, D:D + 1], 1.0).then_inc(gru["init"], 2)
                    dve.wait_ge(gru["init"], 2)
                    for h in range(2):
                        dve.wait_ge(fetched[2][h], 16 * (NB // 2))
                    divide(dve, chain, t["got"], D + 1, t["over"])
                    link(V.tensor_tensor(t["sq"][:], t["got"][:, :, 0:D], wide(t["over"]), ALU.mult))

                    def stage_block(b, r, u):
                        if later(b, 2):
                            dve.wait_ge(*gru["turned"].done(b - 2))
                            dve.wait_ge(*gru["block"].done(b - 2))
                        V.tensor_copy(two[:, u, 0:1, 0:D], X[:, bass.ds(b, 1), :]).then_inc(gru["block"].sem, 1)
                        V.tensor_copy(two[:, u, 1:2, 0:D], t["sq"][:, bass.ds(b, 1), :]).then_inc(gru["block"].sem, 1)

                    def keep(b, r, u):
                        dve.wait_ge(*gru["turned"].done(b))
                        if later(b, 2):
                            dve.wait_ge(*gru["made"].done(b - 2))
                        V.tensor_copy(two_t[:, u].rearrange("p i n -> p (i n)"),
                                      ps[2 + u][:, 0:2 * P]).then_inc(gru["kept"].sem, 1)

                    def reset(b, r, u):
                        dve.wait_ge(*gru["sig"].done(b))
                        if later(b, 2):
                            dve.wait_ge(*gru["tanh"].done(b - 2))
                            dve.wait_ge(*gru["new"].done(b - 2))
                        V.tensor_scalar(gates1[:, u, :], gates[:, u, :], 0.5, 0.5, ALU.mult,
                                        ALU.add).then_inc(gru["part"].sem, 4)
                        dve.wait_ge(*gru["part"].done(b))
                        V.tensor_tensor(cand[:, u, :], gates1[:, u, 0:D], ps[4 + u][:, 3 * D:4 * D],
                                        ALU.mult).then_inc(gru["reset"].sem, 1)
                        dve.wait_ge(*gru["reset"].part(b, 1))
                        V.tensor_tensor(cand[:, u, :], cand[:, u, :], ps[4 + u][:, 2 * D:3 * D],
                                        ALU.add).then_inc(gru["reset"].sem, 1)

                    def update(b, r, u):
                        dve.wait_ge(*gru["tanh"].done(b))
                        nw = gru["new"]
                        V.tensor_tensor(gates[:, u, 0:D], ps[4 + u][:, 4 * D:GW], cand[:, u, :],
                                        ALU.subtract).then_inc(nw.sem, 1)
                        dve.wait_ge(*nw.part(b, 1))
                        V.tensor_tensor(gates[:, u, 0:D], gates[:, u, 0:D], gates1[:, u, D:2 * D],
                                        ALU.mult).then_inc(nw.sem, 1)
                        dve.wait_ge(*nw.part(b, 2))
                        V.tensor_tensor(t["Y"][:, bass.ds(b, 1), :], gates[:, u, None, 0:D], cand[:, u, None, :],
                                        ALU.add).then_inc(nw.sem, 1)

                    steps_of(dve, NB, 2, [(2, update), (1, keep), (0, stage_block), (1, reset)])
                    dve.wait_ge(*gru["new"].done(NB - 1))
                    link(V.tensor_scalar(t["mean"][:], t["got"][:, :, D], 0.0, None, ALU.is_gt))
                    link(V.tensor_copy(own[:], t["mean"][:]))
                    link(V.tensor_copy(t["sq"][:], X[:]))
                    link(V.copy_predicated(t["sq"][:], own[:, :, None].to_broadcast([P, NB, D]), t["Y"][:]))
                    link(V.tensor_tensor(t["Y"][:], t["sq"][:], X[:], ALU.add))
                    norm_vector(dve, chain, 2, t["Y"], (t["sq"], t["mean"], t["var"]))

        far3_turned, far3_kept, near3_made, z3_ready = sem("far3_turned"), sem("far3_kept"), sem("near3_made"), \
            sem("z3_ready")
        w3_loaded = sem("w3_loaded")
        with ExitStack() as ctx:
            Z3 = sbt(ctx, "Z3", [P, NB, D + 1])
            prod = sbt(ctx, "prod", [P, NB, D])
            far3 = sbt(ctx, "far3", [P, NB])
            far3_t = sbt(ctx, "far3_t", [NB, P])
            w3 = sbt(ctx, "w3", [P, 2, D])
            b3 = sbt(ctx, "b3", [P, 1])
            chain = Chain(sem("node_chain3a"))
            with nc.Block() as block:
                @block.sync
                def _(sp):
                    sp.dma_start(w3[:].rearrange("p e f -> p (e f)"),
                                 A["w3"].to_broadcast([P, 2 * D])).then_inc(w3_loaded, 16)
                    sp.dma_start(b3[:], A["b3"][None, :].to_broadcast([P, 1])).then_inc(w3_loaded, 16)
                    sp.wait_ge(z3_ready, 1)
                    sp.dma_start(table[3].rearrange("(b p) w -> p b w", p=P), Z3[:]).then_inc(stored, 16)
                    sp.wait_ge(stored, 48)

                @block.vector
                def _(dve):
                    link = lambda ins: chain.link(dve, ins)
                    dve.wait_ge(w3_loaded, 32)
                    link(V.tensor_copy(Z3[:, :, 0:D], X[:]))
                    link(V.tensor_tensor(prod[:], X[:], row3(w3[:, 0, :]), ALU.mult))
                    V.tensor_reduce(Z3[:, :, D:D + 1], prod[:], AX, ALU.add).then_inc(z3_ready, 1)
                    dve.wait_ge(z3_ready, 1)
                    link(V.tensor_tensor(prod[:], X[:], row3(w3[:, 1, :]), ALU.mult))
                    link(V.tensor_reduce(far3[:], prod[:], AX, ALU.add))
                    V.tensor_scalar(far3[:], far3[:], b3[:, 0:1], None, ALU.add).then_inc(far3_turned, 1)
                    near_vector(dve, chain, far3_turned, far3_t, far3_kept, near3_made)

                @block.tensor
                def _(pe):
                    near_tensor(pe, far3, far3_turned, far3_t, far3_kept, near3_made)

        edge_layer(3, "d", "plain")
        with ExitStack() as ctx:
            t = node_tiles(ctx, 3, D + 1)
            chain = Chain(sem("node_chain3"))
            with nc.Block() as block:
                @block.sync
                def _(sp):
                    fetch(sp, 3, "d", 0, t["got"], D + 1)
                    sp.wait_ge(xs_ready[3], 1)
                    sp.dma_start(out[0:(NB - 1) * P, :].rearrange("(b p) f -> p b f", p=P),
                                 X[:, 0:NB - 1, :]).then_inc(stored, 16)
                    sp.dma_start(out[(NB - 1) * P:, :], X[0:LASTN, NB - 1, :]).then_inc(stored, 16)
                    sp.wait_ge(stored, 16 * 5)

                @block.scalar
                def _(act):
                    fetch(act, 3, "d", 1, t["got"], D + 1)
                    norm_scalar(act, 3, t["var"])

                @block.vector
                def _(dve):
                    link = lambda ins: chain.link(dve, ins)
                    for h in range(2):
                        dve.wait_ge(fetched[3][h], 16 * (NB // 2))
                    divide(dve, chain, t["got"], D + 1, t["over"])
                    link(V.tensor_tensor(t["Y"][:], t["got"][:, :, 0:D], wide(t["over"]), ALU.mult))
                    link(V.tensor_tensor(t["Y"][:], t["Y"][:], X[:], ALU.add))
                    norm_vector(dve, chain, 3, t["Y"], (t["sq"], t["mean"], t["var"]))


_SHAPES = dict(x="x", src="src", dst="dst", edge_attr_16="e16", edge_attr_2="e2", L0_gnn_W_fc="w_fc",
               L0_gnn_W_attn="w_attn", L0_gnn_W_edge="w_edge", L0_gnn_W_e2n="w_e2n", L0_gnn_W_m1="w_m1",
               L0_gnn_W_m2="w_m2", L2_gnn_W_att1="w_att1", L2_gnn_b_att1="b_att1", L2_gnn_W_att2="w_att2",
               L2_gnn_b_att2="b_att2", L2_gnn_W_lin="w_lin", L2_gnn_b_lin="b_lin", L2_gnn_W_ih="w_ih",
               L2_gnn_b_ih="b_ih", L2_gnn_W_hh="w_hh", L2_gnn_b_hh="b_hh", L3_gnn_W="w3", L3_gnn_b="b3")
_TRANSPOSED = ("w_fc", "w_e2n", "w_att1", "w_lin", "w_ih", "w_hh")


def kernel(**inputs):
    import numpy as np
    import concourse.bacc as bacc
    from concourse.bass_utils import run_bass_kernel_spmd

    nc = bacc.Bacc("TRN2", target_bir_lowering=False, num_devices=1)
    arrays, A = {}, {}

    def give(name, a):
        a = np.ascontiguousarray(a)
        arrays["in_" + name] = a
        A[name] = nc.dram_tensor("in_" + name, a.shape, mybir.dt.from_np(a.dtype), kind="ExternalInput").ap()

    for name, short in _SHAPES.items():
        a = np.asarray(inputs[name])
        give(short, a)
        if short in _TRANSPOSED:
            give(short + "_t", a.T)
    attn = np.asarray(inputs["L0_gnn_W_attn"])
    give("attn_cols", attn[0, :2 * K3 * D].reshape(2 * K3, D).T)
    give("attn_edge", attn[0, 2 * K3 * D:].reshape(E2, 1))
    out = nc.dram_tensor("out", (NODES, D), F32, kind="ExternalOutput").ap()
    build(nc, A, out)
    r = run_bass_kernel_spmd(nc, [arrays], core_ids=[0])
    return r.results[0]["out"]
```

```python
from contextlib import ExitStack

import concourse.bass as bass
from concourse import mybir

F32 = mybir.dt.float32
BF16 = mybir.dt.bfloat16
I32 = mybir.dt.int32
ALU = mybir.AluOpType
ACT = mybir.ActivationFunctionType
AX = mybir.AxisListType.X

P = 128
NODES, D = 12500, 64
EDGES = 200000
NB = -(-NODES // P)
LASTN = NODES - (NB - 1) * P
EP, EK = 125, 1600
G = 4
SLOTS = 4
T = -(-((EDGES + NB * (P - 1)) // P) // (G * 8)) * G * 8
STEPS = T // G
RING = 8
SSTEPS = EK // G
TQ = T // 4
EQ = EK // 4
BIG = 2.0 ** 100
CUT = 2.0 ** 120
SLOPE = 0.01
EPS = 1e-5
E2, E16 = 2, 16
REC = {"d": 2 + E2, "s": 2 + E16}
H1 = 2 * D + E16
RW = D + E2 + 1
K3 = 3


def later(s, k):
    return s >= k if isinstance(s, int) else True


class Stage:

    def __init__(self, sem, k, base=0):
        self.sem, self.k, self.base = sem, k, base

    def done(self, s):
        return self.sem, (s + 1) * self.k + self.base

    def part(self, s, j):
        return self.sem, s * self.k + j + self.base


class Chain:

    def __init__(self, sem):
        self.sem, self.n = sem, 0

    def link(self, eng, ins):
        self.n += 1
        ins.then_inc(self.sem, 1)
        eng.wait_ge(self.sem, self.n)


def steps_of(eng, n, unroll, stages):
    lag = max(l for l, _ in stages)

    def one(t, r, j):
        for l, fn in stages:
            s = t - l
            if isinstance(s, int) and not 0 <= s < n:
                continue
            fn(s, r + (j - l) // unroll, (j - l) % unroll)

    first, last = 2 * unroll, n // unroll * unroll
    for t in range(min(first, n)):
        one(t, t // unroll, t % unroll)
    if last > first:
        with eng.Fori(2, last // unroll) as i:
            for j in range(unroll):
                one(i * unroll + j, i, j)
    for t in range(max(last, first), n + lag):
        one(t, t // unroll, t % unroll)


def build(nc, A, out):
    V, PE, AC, GP = nc.vector, nc.tensor, nc.scalar, nc.gpsimd
    with ExitStack() as top:
        def sbt(ctx, name, shape, dt=F32):
            return ctx.enter_context(nc.sbuf_tensor(name, shape, dt))

        def sem(name):
            return top.enter_context(nc.semaphore(name))

        shared = {}

        def again(name, k, n):
            if name not in shared:
                shared[name] = [sem(name), 0]
            st = Stage(shared[name][0], k, shared[name][1])
            shared[name][1] += k * n
            return st

        def dram(name, shape, dt=F32):
            return nc.dram_tensor(name, shape, dt).ap()

        rec = {k: dram(f"rec_{k}", (P * T, REC[k])) for k in "ds"}
        table = [dram(f"table{l}", (NB * P, w)) for l, w in enumerate((D + 1, D, D, D + 1))]
        sums = [dram(f"sums{l}", ((STEPS + 1) * P, G * RW)) for l in range(4)]

        ps = [top.enter_context(nc.psum_tensor(f"bank{i}", [P, 512], F32)) for i in range(8)]

        iota_f = sbt(top, "iota_f", [P, P])
        iota_b = sbt(top, "iota_b", [P, P], BF16)
        iota_col = sbt(top, "iota_col", [P, 1])
        ident = sbt(top, "ident", [P, P])
        ident_b = sbt(top, "ident_b", [P, P], BF16)
        ones = sbt(top, "ones", [P, P])
        X = sbt(top, "X", [P, NB, D])
        carry = {k: sbt(top, f"carry_{k}", [P, T]) for k in "ds"}
        same = sbt(top, "same", [P, T])
        last = {k: sbt(top, f"last_{k}", [1, 2 * NB], I32) for k in "ds"}
        block_of = sbt(top, "block_of", [1, T], I32)
        pick_d = sbt(top, "pick_d", [P, T])
        near = sbt(top, "near", [P, T])
        ew = sbt(top, "ew", [P, E2])
        w_comb = sbt(top, "w_comb", [P, E2, D])

        consts = Chain(sem("consts"))
        loaded = sem("loaded")

        edges = top.enter_context(ExitStack())
        keys = {k: sbt(edges, f"key_{k}", [EP, EK], I32) for k in "ds"}
        hi = {k: sbt(edges, f"hi_{k}", [EP, EK], BF16) for k in "ds"}
        lo = {k: sbt(edges, f"lo_{k}", [EP, EK]) for k in "ds"}
        row = {k: sbt(edges, f"row_{k}", [EP, EK], I32) for k in "ds"}
        other = {"d": "s", "s": "d"}

        scattering = ExitStack()
        stage = {k: sbt(scattering, f"stage_{k}", [EP, SLOTS, G, REC[k]]) for k in "ds"}
        to_row = {k: sbt(scattering, f"to_row_{k}", [EP, SLOTS, G], I32) for k in "ds"}
        ranking = ExitStack()
        e2_all = sbt(ranking, "e2_all", [EP, EK, E2])
        zeros = sbt(ranking, "zeros", [P, 512])
        before = sbt(ranking, "before", [P, P])
        iota_t = sbt(ranking, "iota_t", [P, T])
        pick_s = sbt(ranking, "pick_s", [P, T])
        pick = {"d": pick_d, "s": pick_s}
        pair = sbt(ranking, "pair", [P, T])
        int_a = sbt(ranking, "int_a", [EP, EK], I32)
        mask = sbt(ranking, "mask", [EP, 2, EK], BF16)
        ranks = sbt(ranking, "ranks", [EP, 2, EK])
        mine = sbt(ranking, "mine", [EP, 2, EK])
        count = sbt(ranking, "count", [EP, NB])
        start_row = sbt(ranking, "start_row", [EP, NB])
        tile = sbt(ranking, "tile", [P, 8])
        tile_i = sbt(ranking, "tile_i", [P, 1], I32)
        filling = ExitStack()
        fill = {"d": sbt(filling, "fill_d", [P, T // 4, REC["d"]]), "s": sbt(filling, "fill_s", [P, T // 16, REC["s"]])}
        filled = sem("filled")
        padded = sem("padded")

        def setup_gpsimd(pool):
            link = lambda ins: consts.link(pool, ins)
            for t in (iota_f, iota_b):
                link(GP.iota(t[:], [[1, P]], base=0, channel_multiplier=0, allow_small_or_imprecise_dtypes=True))
            link(GP.iota(iota_col[:], [[0, 1]], base=0, channel_multiplier=1, allow_small_or_imprecise_dtypes=True))
            link(GP.iota(iota_t[:], [[1, T]], base=0, channel_multiplier=0, allow_small_or_imprecise_dtypes=True))
            link(GP.memset(ones[:], 1.0))
            link(GP.memset(zeros[:], 0.0))
            link(GP.affine_select(out=ident[:], in_=ones[:], compare_op=ALU.is_equal, fill=0.0, base=0,
                                  pattern=[[-1, P]], channel_multiplier=1))
            link(GP.affine_select(out=before[:], in_=ones[:], compare_op=ALU.is_gt, fill=0.0, base=0,
                                  pattern=[[1, P]], channel_multiplier=-1))
            link(GP.tensor_copy(ident_b[:], ident[:]))
            for k in "ds":
                link(GP.memset(fill[k][:], 0.0))
                link(GP.memset(fill[k][:, :, 1:2], -1.0))

        N_CONSTS = 13

        def setup_sync(sp):
            for k, a in (("d", "dst"), ("s", "src")):
                sp.dma_start(keys[k][:], A[a].rearrange("(p k) -> p k", p=EP)).then_inc(loaded, 16)
            sp.dma_start(X[:, 0:NB - 1, :],
                         A["x"][0:(NB - 1) * P, :].rearrange("(b p) f -> p b f", p=P)).then_inc(loaded, 16)
            sp.wait_ge(padded, 1)
            sp.dma_start(X[0:LASTN, NB - 1, :], A["x"][(NB - 1) * P:, :]).then_inc(loaded, 16)
            sp.wait_ge(consts.sem, N_CONSTS)
            for k in "ds":
                n = fill[k].shape[1]
                to = rec[k].rearrange("(p c) w -> p c w", p=P)
                for i in range(T // n):
                    sp.dma_start(to[:, i * n:(i + 1) * n, :], fill[k][:]).then_inc(filled, 16)
            for l in range(4):
                sp.dma_start(sums[l][STEPS * P:, :], zeros[:, 0:G * RW]).then_inc(filled, 16)

            sp.wait_ge(filled, 16 * N_FILLED)

        N_FILLED = 4 + 16 + 4

        digits = Chain(sem("digits"))

        def setup_vector(dve):
            V.memset(X[:, NB - 1, :], 0.0).then_inc(padded, 1)
            dve.wait_ge(loaded, 16 * 4)
            for k in "ds":
                digits.link(dve, V.tensor_scalar(int_a[:], keys[k][:], 7, None, ALU.logical_shift_right))
                digits.link(dve, V.tensor_copy(hi[k][:], int_a[:]))
                digits.link(dve, V.tensor_scalar(int_a[:], keys[k][:], P - 1, None, ALU.bitwise_and))
                digits.link(dve, V.tensor_copy(lo[k][:], int_a[:]))

        rk = {k: dict(counted=Stage(sem(f"counted_{k}"), 1), totals=sem(f"totals_{k}"), tiles=sem(f"tiles_{k}"),
                      starts=sem(f"starts_{k}"), picked=sem(f"picked_{k}"), spread=sem(f"spread_{k}"),
                      spread_read=sem(f"spread_read_{k}"), numbers=sem(f"numbers_{k}"),
                      chain=Chain(sem(f"rank_chain_{k}")),
                      ranked=Stage(sem(f"ranked_{k}"), 3), added=Stage(sem(f"added_{k}"), 4)) for k in "ds"}

        def rank_vector(dve, k):
            m = rk[k]
            link = lambda ins: m["chain"].link(dve, ins)
            dve.wait_ge(consts.sem, N_CONSTS)
            def count_block(b, r, u):
                if later(b, 1):
                    dve.wait_ge(*m["counted"].done(b - 1))
                V.tensor_scalar(mask[:, 0, :], hi[k][:], iota_f[0:EP, bass.ds(b, 1)], 0.0, ALU.is_equal, ALU.add,
                                accum_out=count[:, bass.ds(b, 1)]).then_inc(m["counted"].sem, 1)

            steps_of(dve, NB, 2, [(0, count_block)])
            dve.wait_ge(*m["counted"].done(NB - 1))
            c = lambda i: tile[0:NB, i:i + 1]
            dve.wait_ge(m["totals"], 1)
            link(V.tensor_scalar(c(0), ps[0][0:NB, 0:1], float(P - 1), None, ALU.add))
            link(V.tensor_copy(tile_i[0:NB], c(0)))
            link(V.tensor_scalar(tile_i[0:NB], tile_i[0:NB], 7, None, ALU.logical_shift_right))
            V.tensor_copy(c(1), tile_i[0:NB]).then_inc(m["tiles"], 1)
            dve.wait_ge(m["starts"], 1)
            link(V.tensor_copy(c(2), ps[0][0:NB, 1:2]))
            link(V.tensor_tensor(c(3), c(2), c(1), ALU.add))
            link(V.tensor_scalar(c(4), c(2), float(P), None, ALU.mult))
            link(V.tensor_scalar(c(5), c(1), 0.0, None, ALU.is_gt))
            link(V.tensor_scalar(c(6), c(3), -1.0 - T, None, ALU.add))
            link(V.tensor_tensor(c(6), c(6), c(5), ALU.mult))
            link(V.tensor_scalar(c(6), c(6), float(T), None, ALU.add))
            pk, pr = pick[k][0:NB, :], pair[0:NB, :]
            link(V.tensor_scalar(pr, iota_t[0:NB, :], c(2), None, ALU.is_ge))
            link(V.scalar_tensor_tensor(pk, iota_t[0:NB, :], c(3), pr, ALU.is_lt, ALU.mult))
            link(V.memset(pair[0:NB, 0:1], 0.0))
            V.tensor_tensor(pair[0:NB, 1:T], pick[k][0:NB, 1:T], pick[k][0:NB, 0:T - 1],
                            ALU.mult).then_inc(m["picked"], 1)
            dve.wait_ge(m["spread"], 1)
            link(V.tensor_scalar(start_row[:], ps[1][0:EP, 0:NB], -1.0, None, ALU.add))
            link(V.tensor_copy(int_a[0:1, 0:NB], ps[0][0:1, 0:NB]))
            link(V.tensor_scalar(last[k][:, 0:NB], int_a[0:1, 0:NB], 2, None, ALU.logical_shift_right))
            link(V.tensor_scalar(last[k][:, NB:2 * NB], int_a[0:1, 0:NB], G - 1, None, ALU.bitwise_and))
            for i in range(4):
                q = slice(i * TQ, (i + 1) * TQ)
                if k == "d":
                    link(V.tensor_copy(same[:, q], ps[2 + i][:, 0:TQ]))
                V.tensor_scalar(carry[k][:, q], ps[2 + i][:, 0:TQ], -1.0, CUT, ALU.add,
                                ALU.mult).then_inc(m["spread_read"], 1)
            if k == "s":
                dve.wait_ge(m["numbers"], 1)
                for i in range(4):
                    link(V.tensor_copy(block_of[:, i * TQ:(i + 1) * TQ], ps[2 + i][0:1, 0:TQ]))

            ranked, added = m["ranked"], m["added"]

            def rank_block(b, r, u):
                if later(b, 2):
                    dve.wait_ge(*ranked.done(b - 2))
                    dve.wait_ge(*added.done(b - 2))
                V.tensor_scalar(mask[:, u, :], hi[k][:], iota_f[0:EP, bass.ds(b, 1)], None,
                                ALU.is_equal).then_inc(ranked.sem, 1)
                dve.wait_ge(*ranked.part(b, 1))
                V.tensor_tensor_scan(ranks[:, u, :], mask[:, u, :], zero_row, start_row[:, bass.ds(b, 1)], ALU.add,
                                     ALU.add).then_inc(ranked.sem, 1)
                dve.wait_ge(*ranked.part(b, 2))
                V.tensor_tensor(mine[:, u, :], ranks[:, u, :], mask[:, u, :], ALU.mult).then_inc(ranked.sem, 1)

            zero_row = zeros[0:EP, 0:1].to_broadcast([EP, EK])
            steps_of(dve, NB, 2, [(0, rank_block)])
            dve.wait_ge(*added.done(NB - 1))
            for i in range(4):
                link(V.tensor_copy(row[k][:, i * EQ:(i + 1) * EQ], ps[4 + i][0:EP, 0:EQ]))
            link(V.tensor_scalar(int_a[:], row[k][:], P - 1, None, ALU.bitwise_and))
            link(V.tensor_scalar(row[k][:], row[k][:], 7, None, ALU.logical_shift_right))
            link(V.tensor_copy(ranks[:, 0, :], row[k][:]))
            link(V.scalar_tensor_tensor(row[k][:], int_a[:], float(T), ranks[:, 0, :], ALU.mult, ALU.add))

        def rank_tensor(pe, k):
            m = rk[k]
            c = lambda i: tile[0:NB, i:i + 1]
            pe.wait_ge(consts.sem, N_CONSTS)
            pe.wait_ge(*m["counted"].done(NB - 1))
            PE.matmul(ps[0][0:NB, 0:1], count[:], ones[0:EP, 0:1], start=True, stop=True).then_inc(m["totals"], 1)
            pe.wait_ge(m["tiles"], 1)
            PE.matmul(ps[0][0:NB, 1:2], before[0:NB, 0:NB], c(1), start=True, stop=True).then_inc(m["starts"], 1)
            pe.wait_ge(m["picked"], 1)
            PE.matmul(ps[1][0:EP, 0:NB], c(4).to_broadcast([NB, EP]), ident[0:NB, 0:NB], start=True, stop=False)
            PE.matmul(ps[1][0:EP, 0:NB], before[0:EP, 0:EP], count[:], start=False, stop=True)
            PE.matmul(ps[0][0:1, 0:NB], c(6), ident[0:NB, 0:NB], start=True, stop=True)
            for i in range(4):
                mm = PE.matmul(ps[2 + i][:, 0:TQ], ones[0:NB, :], pair[0:NB, i * TQ:(i + 1) * TQ], start=True,
                               stop=True)
            mm.then_inc(m["spread"], 1)
            pe.wait_ge(m["spread_read"], 4)
            if k == "s":
                for i in range(4):
                    mm = PE.matmul(ps[2 + i][0:1, 0:TQ], iota_col[0:NB, :], pick_s[0:NB, i * TQ:(i + 1) * TQ],
                                   start=True, stop=True)
                mm.then_inc(m["numbers"], 1)
            def add_block(b, r, u):
                pe.wait_ge(*m["ranked"].done(b))
                for i in range(4):
                    PE.matmul(ps[4 + i][0:EP, 0:EQ], ident[0:EP, 0:EP], mine[:, u, i * EQ:(i + 1) * EQ],
                              start=isinstance(b, int) and b == 0, stop=True,
                              skip_group_check=True).then_inc(m["added"].sem, 1)

            steps_of(pe, NB, 2, [(0, add_block)])

        with nc.Block() as block:
            @block.gpsimd
            def _(pool):
                setup_gpsimd(pool)

            @block.sync
            def _(sp):
                setup_sync(sp)

            @block.vector
            def _(dve):
                setup_vector(dve)
                rank_vector(dve, "d")

            @block.tensor
            def _(pe):
                rank_tensor(pe, "d")

        filling.close()

        e2_loaded = sem("e2_loaded")
        e16_loaded = [sem(f"e16_loaded{u}") for u in range(SLOTS)]
        staged = {k: Stage(sem(f"staged_{k}"), 4 if k == "d" else 3) for k in "ds"}
        taken = {k: [sem(f"taken_{k}{u}") for u in range(SLOTS)] for k in "ds"}
        scatters = sem("scatters")

        def stage_scalar(act, k):
            if k == "d":
                act.wait_ge(e2_loaded, 16)
            inc = staged[k].sem

            def one(s, r, u):
                if later(s, SLOTS):
                    act.wait_ge(taken[k][u], r * 16 * G)
                cols = bass.ds(s * G, G)
                AC.copy(stage[k][:, u, :, 0:1].bitcast(I32), keys[other[k]][:, cols, None]).then_inc(inc, 1)
                AC.copy(stage[k][:, u, :, 1:2], lo[k][:, cols, None]).then_inc(inc, 1)
                AC.copy(to_row[k][:, u, :], row[k][:, cols]).then_inc(inc, 1)
                if k == "d":
                    AC.copy(stage[k][:, u, :, 2:4], e2_all[:, cols, :]).then_inc(inc, 1)

            steps_of(act, SSTEPS, SLOTS, [(0, one)])

        def stage_sync(sp, k):
            if k == "d":
                sp.dma_start(e2_all[:], A["e2"].rearrange("(p k) e -> p k e", p=EP)).then_inc(e2_loaded, 16)
                return
            e16 = A["e16"].rearrange("(p k) e -> p k e", p=EP)

            def one(s, r, u):
                if later(s, SLOTS):
                    sp.wait_ge(taken[k][u], r * 16 * G)
                sp.dma_start(stage[k][:, u, :, 2:], e16[:, bass.ds(s * G, G), :]).then_inc(e16_loaded[u], 16)

            steps_of(sp, SSTEPS, SLOTS, [(0, one)])

        def scatter_gpsimd(pool, k):
            def one(s, r, u):
                pool.wait_ge(*staged[k].done(s))
                if k == "s":
                    pool.wait_ge(e16_loaded[u], (r + 1) * 16)
                pool.sem_inc(scatters, 1)
                for g in range(G):
                    GP.indirect_dma_start(rec[k], bass.IndirectOffsetOnAxis(to_row[k][:, u, g:g + 1], 0),
                                          stage[k][:, u, g, :], None).then_inc(taken[k][u], 16)

            steps_of(pool, SSTEPS, SLOTS, [(0, one)])
            for u in range(SLOTS):
                pool.wait_ge(taken[k][u], SSTEPS // SLOTS * 16 * G)

        with nc.Block() as block:
            @block.gpsimd
            def _(pool):
                scatter_gpsimd(pool, "d")

            @block.scalar
            def _(act):
                stage_scalar(act, "d")

            @block.sync
            def _(sp):
                stage_sync(sp, "d")

            @block.vector
            def _(dve):
                rank_vector(dve, "s")

            @block.tensor
            def _(pe):
                rank_tensor(pe, "s")
        ranking.close()

        nodes0 = ExitStack()
        Z = sbt(nodes0, "Z", [P, NB, D + 1])
        far = sbt(nodes0, "far", [P, NB])
        dev = sbt(nodes0, "dev", [P, NB, D])
        power = sbt(nodes0, "power", [P, NB, D])
        degree = {k: sbt(nodes0, f"degree_{k}", [P, NB]) for k in "ds"}
        hot_lo = sbt(nodes0, "hot_lo", [EP, 2, G, P], BF16)
        hot_hi = sbt(nodes0, "hot_hi", [EP, 2, G, NB], BF16)
        x_block = sbt(nodes0, "x_block", [P, 2, P])
        x_turned = sbt(nodes0, "x_turned", [D, 2, P])
        w_fc = sbt(nodes0, "w_fc", [D, D])
        w_z = sbt(nodes0, "w_z", [D, D + 2])
        attn_cols = sbt(nodes0, "attn_cols", [D, 2 * K3])
        attn_edge = sbt(nodes0, "attn_edge", [E2, 1])
        w_edge = sbt(nodes0, "w_edge", [E2, E2])
        w_e2n_t = sbt(nodes0, "w_e2n_t", [E2, D])
        w_m = sbt(nodes0, "w_m", [D, 2, D])
        moment_w = sbt(nodes0, "moment_w", [P, 4, D])
        part = sbt(nodes0, "part", [P, D])
        mean = sbt(nodes0, "mean", [P, D])
        moment = sbt(nodes0, "moment", [P, 4, D])
        root = sbt(nodes0, "root", [P, 4, D])
        sign = sbt(nodes0, "sign", [P, 2, D])
        shift = sbt(nodes0, "shift", [P, 1])
        far_t = sbt(nodes0, "far_t", [NB, P])
        w_loaded = sem("w_loaded")
        weights = dict(made=sem("weights_made"), read=sem("weights_read"))
        hist = {k: dict(hot=Stage(sem(f"hot_{k}"), 2 * G), summed=Stage(sem(f"hist_{k}"), 1)) for k in "ds"}
        zs = dict(block=Stage(sem("z_block"), 1), turned=Stage(sem("z_turned"), 1), kept=Stage(sem("z_kept"), 1),
                  made=Stage(sem("z_made"), 1), out=Stage(sem("z_out"), 2))
        nodes0_chain = Chain(sem("nodes0_chain"))
        partial = Stage(sem("partial"), 1)
        spread_sum = Stage(sem("spread_sum"), 1)
        moments_in, roots_out = sem("moments_in"), sem("roots_out")
        far_turned, far_kept, near_made = sem("far_turned"), sem("far_kept"), sem("near_made")
        z_stored = sem("z_stored")

        def weights_sync(sp):
            for to, a in ((w_fc[:], "w_fc"), (w_z[:, 0:D], "w_fc_t"), (attn_cols[:], "attn_cols"),
                          (attn_edge[:], "attn_edge"), (w_edge[:], "w_edge"), (w_e2n_t[:], "w_e2n_t"),
                          (w_m[:, 0, :], "w_m1"), (w_m[:, 1, :], "w_m2")):
                sp.dma_start(to, A[a]).then_inc(w_loaded, 16)

        N_WEIGHTS = 8
        MOMENT_OF = ((0, 1), (0, 4), (1, 2), (1, 5))

        def weights_tensor(pe):
            pe.wait_ge(w_loaded, 16 * N_WEIGHTS)
            w = ps[7]
            PE.matmul(w[0:D, 0:2], w_fc[:], attn_cols[:, 0:K3 + 1:K3], start=True, stop=True)
            PE.matmul(w[:, 2:4], attn_edge[:].to_broadcast([E2, P]), w_edge[:], start=True, stop=True)
            for j in range(E2):
                PE.matmul(w[:, 4 + j * D:4 + (j + 1) * D], w_edge[:, j:j + 1].to_broadcast([E2, P]), w_e2n_t[:],
                          start=True, stop=True)
            for i, (m, v) in enumerate(MOMENT_OF):
                o = 4 + (E2 + i) * D
                mm = PE.matmul(w[:, o:o + D], attn_cols[:, v:v + 1].to_broadcast([D, P]), w_m[:, m, :], start=True,
                               stop=True)
            mm.then_inc(weights["made"], 1)

        def weights_vector(dve):
            link = lambda ins: nodes0_chain.link(dve, ins)
            dve.wait_ge(weights["made"], 1)
            w = ps[7]
            link(V.tensor_copy(w_z[:, D:D + 2], w[0:D, 0:2]))
            link(V.tensor_copy(ew[:], w[:, 2:4]))
            link(V.tensor_copy(w_comb[:].rearrange("p e f -> p (e f)"), w[:, 4:4 + E2 * D]))
            V.tensor_copy(moment_w[:].rearrange("p m f -> p (m f)"),
                          w[:, 4 + E2 * D:4 + (E2 + 4) * D]).then_inc(weights["read"], 1)

        def hist_vector(dve, k):
            hot, summed = hist[k]["hot"], hist[k]["summed"]

            def one(s, r, u):
                if later(s, 2):
                    dve.wait_ge(*summed.done(s - 2))
                    dve.wait_ge(*hot.done(s - 2))
                for g in range(G):
                    V.tensor_scalar(hot_lo[:, u, g, :], iota_b[0:EP, :], lo[k][:, bass.ds(s * G + g, 1)], None,
                                    ALU.is_equal).then_inc(hot.sem, 1)
                    V.tensor_scalar(hot_hi[:, u, g, :], iota_b[0:EP, 0:NB], hi[k][:, bass.ds(s * G + g, 1)], None,
                                    ALU.is_equal).then_inc(hot.sem, 1)

            steps_of(dve, SSTEPS, 2, [(0, one)])
            dve.wait_ge(*summed.done(SSTEPS - 1))
            nodes0_chain.link(dve, V.tensor_copy(degree[k][:], ps["ds".index(k)][:, 0:NB]))

        def hist_tensor(pe, k):
            hot, summed = hist[k]["hot"], hist[k]["summed"]

            def one(s, r, u):
                pe.wait_ge(*hot.done(s))
                for g in range(G):
                    mm = PE.matmul(ps["ds".index(k)][:, 0:NB], hot_lo[:, u, g, :], hot_hi[:, u, g, :],
                                   start=isinstance(s, int) and s == 0 and g == 0, stop=True, skip_group_check=True)
                mm.then_inc(summed.sem, 1)

            steps_of(pe, SSTEPS, 2, [(0, one)])

        def z_vector(dve):
            nodes0_chain.link(dve, V.memset(x_block[:], 0.0))

            def block(b, r, u):
                if later(b, 2):
                    dve.wait_ge(*zs["turned"].done(b - 2))
                    dve.wait_ge(*zs["block"].done(b - 2))
                V.tensor_copy(x_block[:, u, None, 0:D], X[:, bass.ds(b, 1), :]).then_inc(zs["block"].sem, 1)

            def keep(b, r, u):
                dve.wait_ge(*zs["turned"].done(b))
                if later(b, 2):
                    dve.wait_ge(*zs["made"].done(b - 2))
                V.tensor_copy(x_turned[:, u, :], ps[2 + u][0:D, 0:P]).then_inc(zs["kept"].sem, 1)

            def project(b, r, u):
                dve.wait_ge(*zs["made"].done(b))
                V.tensor_copy(Z[:, bass.ds(b, 1), :], ps[4 + u][:, None, 0:D + 1]).then_inc(zs["out"].sem, 1)
                V.tensor_copy(far[:, bass.ds(b, 1)], ps[4 + u][:, D + 1:D + 2]).then_inc(zs["out"].sem, 1)

            steps_of(dve, NB, 2, [(0, block), (1, keep), (2, project)])
            dve.wait_ge(*zs["out"].done(NB - 1))

        def z_tensor(pe):
            pe.wait_ge(weights["read"], 1)

            def turn(b, r, u):
                pe.wait_ge(*zs["block"].done(b))
                if later(b, 2):
                    pe.wait_ge(*zs["kept"].done(b - 2))
                PE.transpose(ps[2 + u][:, 0:P], x_block[:, u, :], ident[:]).then_inc(zs["turned"].sem, 1)

            def project(b, r, u):
                pe.wait_ge(*zs["kept"].done(b))
                if later(b, 2):
                    pe.wait_ge(*zs["out"].done(b - 2))
                PE.matmul(ps[4 + u][:, 0:D + 2], x_turned[:, u, :], w_z[:], start=True,
                          stop=True).then_inc(zs["made"].sem, 1)

            steps_of(pe, NB, 2, [(0, turn), (1, project)])

        def over_nodes(a):
            return a[:].rearrange("p b f -> p f b")

        def wide(a):
            return a[:, :, None].to_broadcast([P, NB, D])

        def moments_vector(dve):
            link = lambda ins: nodes0_chain.link(dve, ins)
            n = 0

            def total(src, to, n):
                V.tensor_reduce(part[:], over_nodes(src), AX, ALU.add).then_inc(partial.sem, 1)
                dve.wait_ge(*spread_sum.done(n))
                link(V.tensor_scalar(to, ps[6][:, 0:D], 1.0 / EDGES, None, ALU.mult))

            for i, k in enumerate("sd"):
                link(V.tensor_tensor(power[:], Z[:, :, 0:D], wide(degree[k]), ALU.mult))
                total(power, mean[:], n)
                n += 1
                link(V.tensor_tensor(dev[:], Z[:, :, 0:D], mean[:, None, :].to_broadcast([P, NB, D]), ALU.subtract))
                link(V.tensor_tensor(power[:], dev[:], dev[:], ALU.mult))
                link(V.tensor_tensor(power[:], power[:], wide(degree[k]), ALU.mult))
                total(power, moment[:, i, :], n)
                n += 1
                link(V.tensor_tensor(power[:], power[:], dev[:], ALU.mult))
                total(power, moment[:, 2 + i, :], n)
                n += 1
            link(V.tensor_scalar(sign[:], moment[:, 2:4, :], 0.0, None, ALU.is_ge))
            link(V.tensor_scalar(sign[:], sign[:], 2.0, -1.0, ALU.mult, ALU.add))
            link(V.tensor_tensor(moment[:, 2:4, :], moment[:, 2:4, :], sign[:], ALU.mult))
            V.tensor_scalar(moment[:], moment[:], 1e-37, None, ALU.max).then_inc(moments_in, 1)
            dve.wait_ge(roots_out, 3)
            link(V.tensor_tensor(root[:, 2:4, :], root[:, 2:4, :], sign[:], ALU.mult))
            link(V.tensor_tensor(root[:], root[:], moment_w[:], ALU.mult))
            link(V.tensor_reduce(shift[:], root[:].rearrange("p m f -> p (m f)"), AX, ALU.add))
            V.tensor_scalar(far[:], far[:], shift[:, 0:1], None, ALU.add).then_inc(far_turned, 1)
            near_vector(dve, nodes0_chain, far_turned, far_t, far_kept, near_made)

        def near_vector(dve, chain, turned, t, kept, made):
            dve.wait_ge(turned, 2)
            V.tensor_copy(t[:], ps[6][0:NB, 0:P]).then_inc(kept, 1)
            dve.wait_ge(made, 1)
            for i in range(4):
                chain.link(dve, V.tensor_copy(near[:, i * TQ:(i + 1) * TQ], ps[i][:, 0:TQ]))

        def near_tensor(pe, col, turned, t, kept, made):
            pe.wait_ge(turned, 1)
            PE.transpose(ps[6][0:NB, 0:P], col[:], ident[:]).then_inc(turned, 1)
            pe.wait_ge(kept, 1)
            for i in range(4):
                mm = PE.matmul(ps[i][:, 0:TQ], t[:], pick_d[0:NB, i * TQ:(i + 1) * TQ], start=True, stop=True)
            mm.then_inc(made, 1)

        def moments_tensor(pe):
            for n in range(6):
                pe.wait_ge(*partial.done(n))
                PE.matmul(ps[6][:, 0:D], ones[:], part[:], start=True, stop=True).then_inc(spread_sum.sem, 1)
            near_tensor(pe, far, far_turned, far_t, far_kept, near_made)

        def moments_scalar(act):
            act.wait_ge(moments_in, 1)
            AC.sqrt(root[:, 0:2, :], moment[:, 0:2, :]).then_inc(roots_out, 1)
            AC.activation(root[:, 2:4, :], moment[:, 2:4, :], ACT.Ln).then_inc(roots_out, 1)
            act.wait_ge(roots_out, 2)
            AC.activation(root[:, 2:4, :], root[:, 2:4, :], ACT.Exp, scale=1.0 / 3.0).then_inc(roots_out, 1)

        with nc.Block() as block:
            @block.gpsimd
            def _(pool):
                scatter_gpsimd(pool, "s")

            @block.sync
            def _(sp):
                weights_sync(sp)
                stage_sync(sp, "s")
                sp.wait_ge(*zs["out"].done(NB - 1))
                sp.dma_start(table[0].rearrange("(b p) w -> p b w", p=P), Z[:]).then_inc(z_stored, 16)
                sp.wait_ge(z_stored, 16)

            @block.scalar
            def _(act):
                stage_scalar(act, "s")
                moments_scalar(act)

            @block.vector
            def _(dve):
                weights_vector(dve)
                z_vector(dve)
                hist_vector(dve, "d")
                hist_vector(dve, "s")
                moments_vector(dve)

            @block.tensor
            def _(pe):
                weights_tensor(pe)
                z_tensor(pe)
                hist_tensor(pe, "d")
                hist_tensor(pe, "s")
                moments_tensor(pe)

        nodes0.close()
        scattering.close()
        edges.close()

        cleared = Chain(sem("cleared"))

        def edge_layer(l, k, kind, A_all=None, w_in=None, w_out=None, b_out=None):
            soft, gated = kind != "sum", kind == "gated"
            W = {"moments": RW, "sum": D, "gated": D + 1, "plain": D + 1}[kind]
            TW = D + 1 if kind in ("moments", "plain") else D
            VW = D + E16
            SCORE, SPREAD, TOP, MSG, SCALE, SUM = (2, 3, 4, 5, 6, 7) if gated else (2, 2, 3, 4, 5, 5)
            look = 1 if gated else 2
            name = lambda s: f"l{l}_{s}"
            with ExitStack() as ctx:
                buf = lambda n, shape, dt=F32: sbt(ctx, name(n), shape, dt)
                slab = buf("slab", [P, RING, G, REC[k]])
                rows = buf("rows", [P, RING, G, VW])
                hot = buf("hot", [P, RING, G, P])
                kept = buf("kept", [P, RING, G * W])
                if soft:
                    far_off = buf("far_off", [P, RING, G, P], BF16)
                    turned = buf("turned", [P, RING, G, P])
                    score = buf("score", [P, RING, G])
                    at_node = buf("at_node", [P, RING, G, 2])
                    top_ = buf("top", [P, 2, G])
                    best = buf("best", [P, RING * G + 1])
                    gaps = buf("gaps", [P, RING, 2, G])
                    factor = buf("factor", [P, RING, 2, G])
                    arg = buf("arg", [P, RING, 3, G])
                    message = buf("message", [P, RING, G, W])
                    scaled = buf("scaled", [P, 2, G * W])
                if gated:
                    feat = buf("feat", [P, 2, G, P])
                    junk = buf("junk", [P, 2, H1])
                    masked = buf("masked", [P, 2, G, P])
                st = lambda n, c: again(n, c, STEPS)
                ring = lambda n, c: [again(f"{n}{u}", c, STEPS // RING) for u in range(RING)]
                slab_in, rows_in, saved = ring("slab_in", 16), ring("rows_in", 16 * G), ring("saved", 16)
                S = dict(hot=st("hot", 1), agg=st("agg", 1), kept=st("kept", G))
                gathers = again("gathers", 1, STEPS).sem
                wrapped = again("wrapped", 1, STEPS // RING).sem
                if soft:
                    S.update(far=st("far", 1), off=st("off", 1), turned=st("turned", 1),
                             score=st("score", {"moments": 2, "plain": 1, "gated": G + 1}[kind]),
                             spread=st("spread", 1), top=st("top", 1 if gated else 3), own=st("own", 0 if gated else 1),
                             gaps=st("gaps", 4), carried=st("carried", 1), factor=st("factor", 1),
                             arg=st("arg", 2 if gated else 4), weight=st("weight", 1),
                             message=st("message", 2 if kind == "moments" else 1), scaled=st("scaled", 1))
                if gated:
                    S.update(edge=st("edge", 1), flipped=st("flipped", 1), feat=st("feat", 1), hidden=st("hidden", 2),
                             masked=st("masked", 1))
                done = lambda n, s: S[n].done(s)
                SB = 1 if gated else 2
                sum_bank = lambda u: ps[6 + u % SB]
                mask_bank = lambda u: ps[7] if gated else ps[u % 2]
                CB = 1 if gated else 2
                carried_bank = lambda u: ps[2 + u % CB]
                read_last = "message" if soft else "kept"

                def gather_gpsimd(pool):
                    def one(s, r, u):
                        if later(s, RING):
                            pool.wait_ge(*done(read_last, s - RING))
                        pool.wait_ge(*slab_in[u].done(r))
                        pool.sem_inc(gathers, 1)
                        for g in range(G):
                            GP.indirect_dma_start(rows[:, u, g, 0:TW], None, table[l],
                                                  bass.IndirectOffsetOnAxis(slab[:, u, g, 0:1].bitcast(I32), 0)
                                                  ).then_inc(rows_in[u].sem, 16)

                    steps_of(pool, STEPS, RING, [(0, one)])

                def records_sync(sp):
                    src = rec[k].rearrange("(p t) w -> p t w", p=P)

                    def load(s, r, u):
                        if later(s, RING):
                            sp.wait_ge(*done(read_last, s - RING))
                        sp.dma_start(slab[:, u, :, :],
                                     src[:, bass.ds(s * G, G), :]).then_inc(slab_in[u].sem, 16)

                    def save(s, r, u):
                        sp.wait_ge(*done("kept", s))
                        sp.dma_start(sums[l][bass.ds(s * P, P), 0:G * W],
                                     kept[:, u, :]).then_inc(saved[u].sem, 16)

                    steps_of(sp, STEPS, RING, [(0, load), (SUM + 3, save)])
                    for u in range(RING):
                        sp.wait_ge(*saved[u].done(STEPS // RING - 1))

                def edge_vector(dve):
                    cleared.link(dve, V.memset(kept[:, RING - 1, :], 0.0))
                    if soft:
                        cleared.link(dve, V.memset(best[:, 0:1], -CUT))
                    prev = lambda u: (u - 1) % RING

                    def make_hot(s, r, u):
                        if soft and later(s, MSG + 1):
                            dve.wait_ge(*done("message", s - MSG - 1))
                        elif later(s, 1):
                            dve.wait_ge(*done("hot", s - 1))
                        if later(s, RING):
                            dve.wait_ge(*done("agg", s - RING))
                        dve.wait_ge(*slab_in[u].done(r))
                        V.tensor_tensor(hot[:, u], iota_f[:, None, :].to_broadcast([P, G, P]),
                                        slab[:, u, :, 1:2].to_broadcast([P, G, P]),
                                        ALU.is_equal).then_inc(S["hot"].sem, 1)

                    sc = lambda u: score[:, u, :, None]

                    def gated_score(g):
                        def one(s, r, u):
                            if g % 2 == 0:
                                dve.wait_ge(*S["hidden"].part(s, g // 2 + 1))
                            if g >= 2:
                                dve.wait_ge(*S["score"].part(s, g - 1))
                            V.scalar_tensor_tensor(junk[:, g % 2, :], ps[4 + g // 2][:, g % 2 * 256:g % 2 * 256 + H1],
                                                   0.0, w_out[:], ALU.max, ALU.mult,
                                                   accum_out=score[:, u, g:g + 1]).then_inc(S["score"].sem, 1)
                        return one

                    def gated_bias(s, r, u):
                        dve.wait_ge(*S["score"].part(s, G))
                        V.tensor_scalar(score[:, u, :], score[:, u, :], b_out[:, 0:1], None,
                                        ALU.add).then_inc(S["score"].sem, 1)

                    def far_score(s, r, u):
                        dve.wait_ge(*rows_in[u].done(r))
                        if kind == "plain":
                            V.tensor_copy(sc(u), rows[:, u, :, D:D + 1]).then_inc(S["score"].sem, 1)
                        else:
                            V.scalar_tensor_tensor(sc(u), slab[:, u, :, 2:3], ew[:, 0:1], rows[:, u, :, D:D + 1],
                                                   ALU.mult, ALU.add).then_inc(S["score"].sem, 1)

                    def edge_score(s, r, u):
                        dve.wait_ge(*S["score"].part(s, 1))
                        V.scalar_tensor_tensor(sc(u), slab[:, u, :, 3:4], ew[:, 1:2], sc(u), ALU.mult,
                                               ALU.add).then_inc(S["score"].sem, 1)

                    cols = lambda s: bass.ds(s * G, G)
                    shift_of = lambda u: at_node[:, u, :, 1]

                    def tile_max(s, r, u):
                        dve.wait_ge(*done("spread", s))
                        bank = ps[u % 2][:].rearrange("p (g e) -> p g e", g=G)
                        to = at_node[:, u, :, 1:2] if gated else top_[:, 0, :, None]
                        V.tensor_reduce(to, bank, AX, ALU.max).then_inc(S["top"].sem, 1)

                    def max_near(s, r, u):
                        dve.wait_ge(*S["top"].part(s, 1))
                        V.tensor_tensor(top_[:, 1, :], top_[:, 0, :], near[:, cols(s)],
                                        ALU.add).then_inc(S["top"].sem, 1)

                    def max_leaky(s, r, u):
                        dve.wait_ge(*S["top"].part(s, 2))
                        V.scalar_tensor_tensor(at_node[:, u, :, 1:2], top_[:, 1, :, None], SLOPE, top_[:, 1, :, None],
                                               ALU.mult, ALU.max).then_inc(S["top"].sem, 1)

                    before_ = lambda u: best[:, u * G:(u + 1) * G]
                    after_ = lambda u: best[:, u * G + 1:(u + 1) * G + 1]

                    def running_max(s, r, u):
                        dve.wait_ge(*done("top", s))
                        V.tensor_tensor_scan(after_(u), carry[k][:, cols(s)], shift_of(u), best[:, u * G:u * G + 1],
                                             ALU.add, ALU.max).then_inc(S["gaps"].sem, 1)

                    def old_gap(s, r, u):
                        dve.wait_ge(*S["gaps"].part(s, 1))
                        V.tensor_tensor(gaps[:, u, 0, :], before_(u), carry[k][:, cols(s)],
                                        ALU.add).then_inc(S["gaps"].sem, 1)

                    def new_gap(s, r, u):
                        V.tensor_tensor(gaps[:, u, 1, :], shift_of(u), after_(u),
                                        ALU.subtract).then_inc(S["gaps"].sem, 1)

                    def old_gap_less(s, r, u):
                        dve.wait_ge(*S["gaps"].part(s, 3))
                        V.tensor_tensor(gaps[:, u, 0, :], gaps[:, u, 0, :], after_(u),
                                        ALU.subtract).then_inc(S["gaps"].sem, 1)
                        if u == RING - 1:
                            V.tensor_copy(best[:, 0:1], best[:, RING * G:]).then_inc(wrapped, 1)

                    carried = lambda u: carried_bank(u)[:, 0:G * look].rearrange("p (g c) -> p g c", c=look)

                    def arg_near(s, r, u):
                        dve.wait_ge(*done("carried", s))
                        V.tensor_tensor(arg[:, u, 0, :, None], sc(u), carried(u)[:, :, 0:1],
                                        ALU.add).then_inc(S["arg"].sem, 1)

                    def arg_leaky(s, r, u):
                        dve.wait_ge(*S["arg"].part(s, 1))
                        V.scalar_tensor_tensor(arg[:, u, 1, :], arg[:, u, 0, :], SLOPE, arg[:, u, 0, :], ALU.mult,
                                               ALU.max).then_inc(S["arg"].sem, 1)

                    def arg_less(s, r, u):
                        if gated:
                            dve.wait_ge(*done("carried", s))
                            V.tensor_tensor(arg[:, u, 1, :, None], sc(u), carried(u),
                                            ALU.subtract).then_inc(S["arg"].sem, 1)
                            return
                        dve.wait_ge(*S["arg"].part(s, 2))
                        V.tensor_tensor(arg[:, u, 1, :, None], arg[:, u, 1, :, None], carried(u)[:, :, 1:2],
                                        ALU.subtract).then_inc(S["arg"].sem, 1)

                    def arg_capped(s, r, u):
                        dve.wait_ge(*S["arg"].part(s, S["arg"].k - 1))
                        V.tensor_scalar(arg[:, u, 2, :], arg[:, u, 1, :], 1.0, None,
                                        ALU.min).then_inc(S["arg"].sem, 1)

                    def make_message(s, r, u):
                        dve.wait_ge(*done("weight", s))
                        w = message[:, u, :, W - 1:W]
                        V.tensor_tensor(message[:, u, :, 0:D], rows[:, u, :, 0:D], w.to_broadcast([P, G, D]),
                                        ALU.mult).then_inc(S["message"].sem, 1)
                        if kind == "moments":
                            V.tensor_tensor(message[:, u, :, D:D + E2], slab[:, u, :, 2:4],
                                            w.to_broadcast([P, G, E2]), ALU.mult).then_inc(S["message"].sem, 1)

                    def add_sums(g):
                        def one(s, r, u):
                            kp = S["kept"]
                            if g == 0:
                                if later(s, RING):
                                    dve.wait_ge(*saved[u].done(r - 1))
                                dve.wait_ge(*done("scaled" if soft else "agg", s))
                            if g or later(s, 1):
                                dve.wait_ge(*kp.part(s, g))
                            old = kept[:, u, (g - 1) * W:g * W] if g else kept[:, prev(u), (G - 1) * W:]
                            by = factor[:, u, 0, g:g + 1] if soft else same[:, bass.ds(s * G + g, 1)]
                            new = scaled[:, u % 2, g * W:(g + 1) * W] if soft else sum_bank(u)[:, g * W:(g + 1) * W]
                            V.scalar_tensor_tensor(kept[:, u, g * W:(g + 1) * W], old, by, new, ALU.mult,
                                                   ALU.add).then_inc(kp.sem, 1)
                        return one

                    if kind == "gated":
                        order = [(TOP, tile_max), (MSG, arg_less), (TOP, running_max), (MSG, arg_capped),
                                 (TOP, old_gap), (SUM, add_sums(0)), (TOP, new_gap), (SUM, add_sums(1)),
                                 (TOP, old_gap_less), (0, make_hot), (SCORE, gated_score(0)), (SCORE, gated_score(1)),
                                 (SUM, add_sums(2)), (MSG, make_message), (SCORE, gated_score(2)),
                                 (SCORE, gated_score(3)), (SUM, add_sums(3)), (SCORE, gated_bias)]
                    elif soft:
                        order = [(SCORE, far_score), (MSG, arg_near)]
                        order += [(SCORE, edge_score)] if kind == "moments" else []
                        order += [(MSG, arg_leaky), (TOP, tile_max), (MSG, arg_less), (TOP, max_near),
                                  (MSG, arg_capped), (TOP, max_leaky), (0, make_hot), (TOP, running_max),
                                  (SUM, add_sums(0)), (TOP, old_gap), (TOP, new_gap), (SUM, add_sums(1)),
                                  (TOP, old_gap_less), (SUM, add_sums(2)), (MSG, make_message),
                                  (SUM, add_sums(3))]
                    else:
                        order = [(0, make_hot)] + [(1, add_sums(g)) for g in range(G)]
                    steps_of(dve, STEPS, RING, order)

                def edge_tensor(pe):
                    def node_mask(s, r, u):
                        pe.wait_ge(*done("far", s))
                        if gated and later(s, 1):
                            pe.wait_ge(*done("turned", s - 1))
                        if not gated and later(s, 2):
                            pe.wait_ge(*S["top"].part(s - 2, 1))
                        for g in range(G):
                            mm = PE.matmul(mask_bank(u)[:, g * P:(g + 1) * P], far_off[:, u, g, :], ident_b[:],
                                           start=g == 0, stop=False, skip_group_check=True)
                        mm.then_inc(S["off"].sem, 1)

                    def add_scores(s, r, u):
                        pe.wait_ge(*done("score", s))
                        pe.wait_ge(*done("turned", s))
                        for g in range(G):
                            mm = PE.matmul(ps[u % 2][:, g * P:(g + 1) * P],
                                           score[:, u, g:g + 1].to_broadcast([P, P]), ident[:],
                                           start=False, stop=True, skip_group_check=True)
                        mm.then_inc(S["spread"].sem, 1)

                    def turn_scores(s, r, u):
                        pe.wait_ge(*done("masked", s))
                        if later(s, 2):
                            pe.wait_ge(*done("top", s - 2))
                        for g in range(G):
                            mm = PE.matmul(ps[u % 2][:, g * P:(g + 1) * P], masked[:, u % 2, g, :], ident[:],
                                           start=True, stop=True, is_transpose=True, skip_group_check=True)
                        mm.then_inc(S["spread"].sem, 1)

                    def carry_over(s, r, u):
                        pe.wait_ge(*done("top", s))
                        if not gated:
                            pe.wait_ge(*done("own", s))
                        if later(s, CB):
                            pe.wait_ge(*done("arg", s - CB))
                        for g in range(G):
                            mm = PE.matmul(carried_bank(u)[:, g * look:(g + 1) * look], turned[:, u, g, :],
                                           at_node[:, u, g, 2 - look:2], start=True, stop=True,
                                           skip_group_check=True)
                        mm.then_inc(S["carried"].sem, 1)

                    def sum_edges(s, r, u):
                        if soft:
                            pe.wait_ge(*done("message", s))
                            if later(s, SB):
                                pe.wait_ge(*done("scaled", s - SB))
                        else:
                            pe.wait_ge(*done("hot", s))
                            pe.wait_ge(*rows_in[u].done(r))
                            if later(s, 2):
                                pe.wait_ge(*done("kept", s - 2))
                        for g in range(G):
                            rhs = message[:, u, g, :] if soft else rows[:, u, g, 0:D]
                            mm = PE.matmul(sum_bank(u)[:, g * W:(g + 1) * W], hot[:, u, g, :], rhs, start=True,
                                           stop=True, skip_group_check=True)
                        mm.then_inc(S["agg"].sem, 1)

                    def flip(s, r, u):
                        pe.wait_ge(*done("edge", s))
                        pe.wait_ge(*rows_in[u].done(r))
                        if later(s, 1):
                            pe.wait_ge(*done("feat", s - 1))
                        for g in range(G):
                            mm = PE.matmul(ps[3][0:VW, g * P:(g + 1) * P], rows[:, u, g, :], ident[:], start=True,
                                           stop=True, is_transpose=True, skip_group_check=True)
                        mm.then_inc(S["flipped"].sem, 1)

                    def hidden(s, r, u):
                        near_block = [pe.value_load(block_of[0:1, bass.ds(s * G + g, 1)], min_val=0, max_val=NB - 1)
                                      for g in range(G)]
                        pe.wait_ge(*done("feat", s))
                        pe.wait_ge(*done("turned", s))
                        for g in range(G):
                            if g % 2 == 0 and later(s, 1):
                                pe.wait_ge(*S["score"].part(s - 1, g + 2))
                            o = ps[4 + g // 2][:, g % 2 * 256:g % 2 * 256 + H1]
                            PE.matmul(o, feat[0:VW, u % 2, g, :], w_in[0:VW, :], start=True, stop=False,
                                      skip_group_check=True)
                            mm = PE.matmul(o, turned[:, u, g, :], A_all[:, bass.ds(near_block[g], 1), :],
                                           start=False, stop=True, skip_group_check=True)
                            if g % 2 == 1:
                                mm.then_inc(S["hidden"].sem, 1)

                    if gated:
                        steps_of(pe, STEPS, RING, [(SCORE, hidden), (TOP, carry_over), (SPREAD, turn_scores), (1, flip),
                                                   (1, node_mask), (MSG, sum_edges)])
                    elif soft:
                        steps_of(pe, STEPS, RING, [(SPREAD, add_scores), (1, node_mask), (TOP, carry_over),
                                                   (MSG, sum_edges)])
                    else:
                        steps_of(pe, STEPS, RING, [(0, sum_edges)])

                def edge_scalar(act):
                    def node_far(s, r, u):
                        act.wait_ge(*done("hot", s))
                        if later(s, RING):
                            act.wait_ge(*done("spread", s - RING))
                        AC.activation(far_off[:, u], hot[:, u], ACT.Copy, bias=-BIG,
                                      scale=BIG).then_inc(S["far"].sem, 1)

                    def mask_scores(s, r, u):
                        act.wait_ge(*done("score", s))
                        if later(s, 2):
                            act.wait_ge(*done("spread", s - 2))
                        for g in range(G):
                            ins = AC.activation(masked[:, u % 2, g, :], far_off[:, u, g, :], ACT.Identity,
                                                bias=score[:, u, g:g + 1], scale=1.0)
                        ins.then_inc(S["masked"].sem, 1)

                    def own_score(s, r, u):
                        if later(s, RING):
                            act.wait_ge(*done("carried", s - RING))
                        AC.copy(at_node[:, u, :, 0:1], near[:, bass.ds(s * G, G), None]).then_inc(S["own"].sem, 1)

                    def scale_sums(s, r, u):
                        act.wait_ge(*done("agg", s))
                        act.wait_ge(*done("factor", s))
                        if later(s, 2):
                            act.wait_ge(*done("kept", s - 2))
                        for g in range(G):
                            c = slice(g * W, (g + 1) * W)
                            ins = AC.mul(scaled[:, u % 2, c], sum_bank(u)[:, c], factor[:, u, 1, g:g + 1])
                        ins.then_inc(S["scaled"].sem, 1)

                    def turn(s, r, u):
                        act.wait_ge(*done("off", s))
                        if later(s, RING):
                            act.wait_ge(*done("carried", s - RING))
                        AC.activation(turned[:, u].rearrange("p g e -> p (g e)"), mask_bank(u)[:], ACT.Relu,
                                      bias=1.0, scale=1.0 / BIG).then_inc(S["turned"].sem, 1)

                    def edge_features(s, r, u):
                        act.wait_ge(*slab_in[u].done(r))
                        if later(s, RING):
                            act.wait_ge(*done("message", s - RING))
                        AC.copy(rows[:, u, :, D:VW], slab[:, u, :, 2:]).then_inc(S["edge"].sem, 1)

                    def keep_flipped(s, r, u):
                        act.wait_ge(*done("flipped", s))
                        if later(s, 2):
                            act.wait_ge(*done("hidden", s - 2))
                        AC.copy(feat[0:VW, u % 2].rearrange("p g e -> p (g e)"),
                                ps[3][0:VW, :]).then_inc(S["feat"].sem, 1)

                    def factors(s, r, u):
                        act.wait_ge(*done("gaps", s))
                        if later(s, RING):
                            act.wait_ge(*done("kept", s - RING))
                        AC.activation(factor[:, u], gaps[:, u], ACT.Exp).then_inc(S["factor"].sem, 1)

                    def weight(s, r, u):
                        act.wait_ge(*done("arg", s))
                        if later(s, RING):
                            act.wait_ge(*done("agg", s - RING))
                        AC.activation(message[:, u, :, W - 1:W], arg[:, u, 2, :, None],
                                      ACT.Exp).then_inc(S["weight"].sem, 1)

                    if gated:
                        steps_of(act, STEPS, RING, [(SPREAD, mask_scores), (MSG, weight), (SCALE, scale_sums), (TOP, factors),
                                                    (0, edge_features), (0, node_far), (1, keep_flipped), (1, turn)])
                    else:
                        steps_of(act, STEPS, RING, [(SCALE, scale_sums), (0, own_score), (MSG, weight), (1, turn),
                                                    (0, node_far), (TOP, factors)])

                with nc.Block() as block:
                    @block.gpsimd
                    def _(pool):
                        gather_gpsimd(pool)

                    @block.sync
                    def _(sp):
                        records_sync(sp)

                    @block.vector
                    def _(dve):
                        edge_vector(dve)

                    @block.tensor
                    def _(pe):
                        edge_tensor(pe)

                    if soft:
                        @block.scalar
                        def _(act):
                            edge_scalar(act)

        fetched = [Stage(sem(f"fetched{h}"), 16 * (NB // 2)) for h in range(2)]

        def fetch(eng, l, k, half, to, W):
            src = sums[l].rearrange("(s p) w -> s p w", p=P)[:, :, 0:G * W].rearrange("s p (g w) -> s p g w", g=G)
            lo_b, hi_b = half * (NB // 2), (half + 1) * (NB // 2)
            with eng.Fori(lo_b, hi_b) as b:
                step = eng.value_load(last[k][0:1, bass.ds(b, 1)], min_val=0, max_val=STEPS)
                place = eng.value_load(last[k][0:1, bass.ds(b + NB, 1)], min_val=0, max_val=G - 1)
                eng.dma_start(to[:, bass.ds(b, 1), :],
                              src[bass.ds(step, 1), :, bass.ds(place, 1), :].rearrange("s p g w -> (s p) g w")
                              ).then_inc(fetched[half].sem, 16)
            eng.wait_ge(*fetched[half].done(l))

        eps = sbt(top, "eps", [P, 1])
        norm_var, norm_root = sem("norm_var"), sem("norm_root")

        def norm_vector(dve, chain, l, Y, ctx_tiles):
            sq, mean_n, var_n = ctx_tiles
            link = lambda ins: chain.link(dve, ins)
            link(V.memset(eps[:], EPS))
            link(V.tensor_reduce(mean_n[:], Y[:], AX, ALU.add))
            link(V.tensor_scalar(mean_n[:], mean_n[:], 1.0 / D, None, ALU.mult))
            link(V.tensor_tensor(Y[:], Y[:], wide(mean_n), ALU.subtract))
            link(V.tensor_tensor(sq[:], Y[:], Y[:], ALU.mult))
            V.tensor_reduce(var_n[:], sq[:], AX, ALU.add).then_inc(norm_var, 1)
            dve.wait_ge(norm_root, l + 1)
            link(V.reciprocal(var_n[:], var_n[:]))
            V.tensor_tensor(X[:], Y[:], wide(var_n), ALU.mult).then_inc(x_ready, 1)
            dve.wait_ge(x_ready, l + 1)

        def norm_scalar(act, l, var_n):
            act.wait_ge(norm_var, l + 1)
            AC.activation(var_n[:], var_n[:], ACT.Sqrt, bias=eps[:], scale=1.0 / D).then_inc(norm_root, 1)

        def divide(dve, chain, all_, W, over):
            link = lambda ins: chain.link(dve, ins)
            w = all_[:, :, W - 1]
            link(V.tensor_scalar(over[:], w, 0.0, None, ALU.is_equal))
            link(V.tensor_tensor(over[:], over[:], w, ALU.add))
            link(V.reciprocal(over[:], over[:]))

        def node_tiles(ctx, l, W):
            return dict(got=sbt(ctx, f"got{l}", [P, NB, W]), Y=sbt(ctx, f"Y{l}", [P, NB, D]),
                        sq=sbt(ctx, f"sq{l}", [P, NB, D]), mean=sbt(ctx, f"mean{l}", [P, NB]),
                        var=sbt(ctx, f"var{l}", [P, NB]), over=sbt(ctx, f"over{l}", [P, NB]))

        stored = sem("stored")
        x_ready = sem("x_ready")
        node_chain = Chain(sem("node_chain"))
        row3 = lambda a: a[:, None, :].to_broadcast([P, NB, D])

        edge_layer(0, "d", "moments")
        with ExitStack() as ctx:
            t = node_tiles(ctx, 0, RW)
            chain = node_chain
            with nc.Block() as block:
                @block.sync
                def _(sp):
                    fetch(sp, 0, "d", 0, t["got"], RW)
                    sp.wait_ge(x_ready, 1)
                    sp.dma_start(table[1].rearrange("(b p) w -> p b w", p=P), X[:]).then_inc(stored, 16)
                    sp.wait_ge(stored, 16)

                @block.scalar
                def _(act):
                    fetch(act, 0, "d", 1, t["got"], RW)
                    norm_scalar(act, 0, t["var"])

                @block.vector
                def _(dve):
                    link = lambda ins: chain.link(dve, ins)
                    for h in range(2):
                        dve.wait_ge(*fetched[h].done(0))
                    divide(dve, chain, t["got"], RW, t["over"])
                    link(V.tensor_tensor(t["Y"][:], t["got"][:, :, D:D + 1].to_broadcast([P, NB, D]),
                                         row3(w_comb[:, 0, :]), ALU.mult))
                    link(V.tensor_tensor(t["sq"][:], t["got"][:, :, D + 1:D + 2].to_broadcast([P, NB, D]),
                                         row3(w_comb[:, 1, :]), ALU.mult))
                    link(V.tensor_tensor(t["Y"][:], t["Y"][:], t["sq"][:], ALU.add))
                    link(V.tensor_tensor(t["Y"][:], t["Y"][:], t["got"][:, :, 0:D], ALU.add))
                    link(V.tensor_tensor(t["Y"][:], t["Y"][:], wide(t["over"]), ALU.mult))
                    link(V.tensor_tensor(t["Y"][:], t["Y"][:], X[:], ALU.add))
                    norm_vector(dve, chain, 0, t["Y"], (t["sq"], t["mean"], t["var"]))

        edge_layer(1, "d", "sum")
        with ExitStack() as ctx:
            t = node_tiles(ctx, 1, D)
            chain = node_chain
            with nc.Block() as block:
                @block.sync
                def _(sp):
                    fetch(sp, 1, "d", 0, t["got"], D)
                    sp.wait_ge(x_ready, 2)
                    sp.dma_start(table[2].rearrange("(b p) w -> p b w", p=P), X[:]).then_inc(stored, 16)
                    sp.wait_ge(stored, 32)

                @block.scalar
                def _(act):
                    fetch(act, 1, "d", 1, t["got"], D)
                    norm_scalar(act, 1, t["var"])

                @block.vector
                def _(dve):
                    for h in range(2):
                        dve.wait_ge(*fetched[h].done(1))
                    chain.link(dve, V.tensor_tensor(t["Y"][:], t["got"][:], X[:], ALU.add))
                    norm_vector(dve, chain, 1, t["Y"], (t["sq"], t["mean"], t["var"]))

        gated = ExitStack()
        w_in = sbt(gated, "w_in", [D + E16, H1])
        w_near = sbt(gated, "w_near", [D + 1, H1])
        w_out = sbt(gated, "w_out", [P, H1])
        b_out = sbt(gated, "b_out", [P, 1])
        A_all = sbt(gated, "A_all", [P, NB, H1])
        w2_loaded = sem("w2_loaded")

        pre = dict(block=Stage(sem("a_block"), 1), turned=Stage(sem("a_turned"), 1), kept=Stage(sem("a_kept"), 1),
                   made=Stage(sem("a_made"), 1), out=Stage(sem("a_out"), 1), init=sem("a_init"))
        with ExitStack() as ctx:
            b_block = sbt(ctx, "b_block", [P, 2, P])
            b_turned = sbt(ctx, "b_turned", [P, 2, P])
            with nc.Block() as block:
                @block.sync
                def _(sp):
                    for to, a in ((w_in[0:D, :], A["w_att1_t"][D + E16:, :]), (w_in[D:, :], A["w_att1_t"][D:D + E16, :]),
                                  (w_near[0:D, :], A["w_att1_t"][0:D, :]), (w_near[D:, :], A["b_att1"][None, :]),
                                  (w_out[:], A["w_att2"].to_broadcast([P, H1])),
                                  (b_out[:], A["b_att2"][None, :].to_broadcast([P, 1]))):
                        sp.dma_start(to, a).then_inc(w2_loaded, 16)
                    sp.wait_ge(w2_loaded, 16 * 6)

                @block.vector
                def _(dve):
                    V.memset(b_block[:], 0.0).then_inc(pre["init"], 1)
                    dve.wait_ge(pre["init"], 1)
                    V.memset(b_block[:, :, D:D + 1], 1.0).then_inc(pre["init"], 1)
                    dve.wait_ge(pre["init"], 2)

                    def stage_block(b, r, u):
                        if later(b, 2):
                            dve.wait_ge(*pre["turned"].done(b - 2))
                            dve.wait_ge(*pre["block"].done(b - 2))
                        V.tensor_copy(b_block[:, u, None, 0:D], X[:, bass.ds(b, 1), :]).then_inc(pre["block"].sem, 1)

                    def keep(b, r, u):
                        dve.wait_ge(*pre["turned"].done(b))
                        if later(b, 2):
                            dve.wait_ge(*pre["made"].done(b - 2))
                        V.tensor_copy(b_turned[:, u, :], ps[2 + u][:, 0:P]).then_inc(pre["kept"].sem, 1)

                    def drain(b, r, u):
                        dve.wait_ge(*pre["made"].done(b))
                        V.tensor_copy(A_all[:, bass.ds(b, 1), :], ps[4 + u][:, None, 0:H1]).then_inc(pre["out"].sem, 1)

                    steps_of(dve, NB, 2, [(0, stage_block), (1, keep), (2, drain)])

                @block.tensor
                def _(pe):
                    pe.wait_ge(w2_loaded, 16 * 6)
                    pe.wait_ge(pre["init"], 2)

                    def turn(b, r, u):
                        pe.wait_ge(*pre["block"].done(b))
                        if later(b, 2):
                            pe.wait_ge(*pre["kept"].done(b - 2))
                        PE.transpose(ps[2 + u][:, 0:P], b_block[:, u, :], ident[:]).then_inc(pre["turned"].sem, 1)

                    def project(b, r, u):
                        pe.wait_ge(*pre["kept"].done(b))
                        if later(b, 2):
                            pe.wait_ge(*pre["out"].done(b - 2))
                        PE.matmul(ps[4 + u][:, 0:H1], b_turned[0:D + 1, u, :], w_near[:], start=True,
                                  stop=True).then_inc(pre["made"].sem, 1)

                    steps_of(pe, NB, 2, [(0, turn), (1, project)])

        edge_layer(2, "s", "gated", A_all, w_in, w_out, b_out)
        gated.close()

        GW = 5 * D
        gru = dict(block=Stage(sem("g_block"), 2), turned=Stage(sem("g_turned"), 2), kept=Stage(sem("g_kept"), 1),
                   made=Stage(sem("g_made"), 1), sig=Stage(sem("g_sig"), 1), part=Stage(sem("g_part"), 4),
                   reset=Stage(sem("g_reset"), 2), tanh=Stage(sem("g_tanh"), 1), new=Stage(sem("g_new"), 3),
                   init=sem("g_init"), w=sem("g_w"), made_w=sem("g_made_w"), scaled=sem("g_scaled"))
        with ExitStack() as ctx:
            t = node_tiles(ctx, 2, D + 1)
            w_x = sbt(ctx, "w_x", [D + 1, 3 * D])
            w_msg = sbt(ctx, "w_msg", [D + 1, 4 * D])
            w_hh_t = sbt(ctx, "w_hh_t", [D, 3 * D])
            w_lin = sbt(ctx, "w_lin", [D, D + 1])
            two = sbt(ctx, "two", [P, 2, 2, P])
            two_t = sbt(ctx, "two_t", [P, 2, 2, P])
            gates = sbt(ctx, "gates", [P, 2, 2 * D])
            gates1 = sbt(ctx, "gates1", [P, 2, 2 * D])
            cand = sbt(ctx, "cand", [P, 2, D])
            own = sbt(ctx, "own", [P, NB], I32)
            chain = node_chain
            with nc.Block() as block:
                @block.sync
                def _(sp):
                    for to, a in ((w_x[0:D, :], A["w_ih_t"]), (w_x[D:, :], A["b_ih"][None, :]),
                                  (w_hh_t[:], A["w_hh_t"]), (w_lin[:, 0:D], A["w_lin"]),
                                  (w_lin[:, D:], A["b_lin"][:, None]), (w_msg[0:D, 3 * D:], A["w_lin_t"]),
                                  (w_msg[D:, 3 * D:], A["b_lin"][None, :]), (cand[D:D + 1, :, :],
                                  A["b_hh"][0:2 * D].rearrange("(o a f) -> o a f", o=1, a=2)),
                                  (gates[D:D + 1, 0, 0:D], A["b_hh"][None, 2 * D:])):
                        sp.dma_start(to, a).then_inc(gru["w"], 16)
                    fetch(sp, 2, "s", 0, t["got"], D + 1)

                @block.scalar
                def _(act):
                    fetch(act, 2, "s", 1, t["got"], D + 1)

                    def sigmoid_half(b, r, u):
                        act.wait_ge(*gru["made"].done(b))
                        if later(b, 2):
                            act.wait_ge(*gru["new"].done(b - 2))
                        AC.activation(gates[:, u, :], ps[4 + u][:, 0:2 * D], ACT.Tanh,
                                      scale=0.5).then_inc(gru["sig"].sem, 1)

                    def candidate(b, r, u):
                        act.wait_ge(*gru["reset"].done(b))
                        AC.activation(cand[:, u, :], cand[:, u, :], ACT.Tanh).then_inc(gru["tanh"].sem, 1)

                    steps_of(act, NB, 2, [(1, sigmoid_half), (2, candidate)])
                    norm_scalar(act, 2, t["var"])

                @block.tensor
                def _(pe):
                    pe.wait_ge(gru["w"], 16 * 9)
                    PE.matmul(ps[0][0:D + 1, 0:3 * D], w_lin[:], w_hh_t[:], start=True,
                              stop=True).then_inc(gru["made_w"], 1)
                    pe.wait_ge(gru["init"], 2)

                    def turn(b, r, u):
                        pe.wait_ge(*gru["block"].done(b))
                        if later(b, 2):
                            pe.wait_ge(*gru["kept"].done(b - 2))
                        for i in range(2):
                            PE.transpose(ps[2 + u][:, i * P:(i + 1) * P], two[:, u, i, :],
                                         ident[:]).then_inc(gru["turned"].sem, 1)

                    def project(b, r, u):
                        pe.wait_ge(*gru["kept"].done(b))
                        if later(b, 2):
                            pe.wait_ge(*gru["new"].done(b - 2))
                        o = ps[4 + u]
                        PE.matmul(o[:, 0:3 * D], two_t[0:D + 1, u, 0, :], w_x[:], start=True, stop=False,
                                  skip_group_check=True)
                        PE.matmul(o[:, 0:2 * D], two_t[0:D + 1, u, 1, :], w_msg[:, 0:2 * D], start=False, stop=True,
                                  skip_group_check=True)
                        PE.matmul(o[:, 3 * D:GW], two_t[0:D + 1, u, 1, :], w_msg[:, 2 * D:], start=False, stop=True,
                                  skip_group_check=True).then_inc(gru["made"].sem, 1)

                    steps_of(pe, NB, 2, [(0, turn), (1, project)])

                @block.vector
                def _(dve):
                    link = lambda ins: chain.link(dve, ins)
                    dve.wait_ge(gru["made_w"], 1)
                    link(V.tensor_copy(w_msg[0:D, 0:3 * D], ps[0][0:D, 0:3 * D]))
                    link(V.tensor_tensor(w_msg[D:D + 1, 0:2 * D], ps[0][D:D + 1, 0:2 * D],
                                         cand[D:D + 1, :, :].rearrange("p a f -> p (a f)"), ALU.add))
                    link(V.tensor_tensor(w_msg[D:D + 1, 2 * D:3 * D], ps[0][D:D + 1, 2 * D:3 * D],
                                         gates[D:D + 1, 0, 0:D], ALU.add))
                    link(V.memset(two[:], 0.0))
                    V.memset(two[:, :, :, D:D + 1], 1.0).then_inc(gru["init"], 2)
                    dve.wait_ge(gru["init"], 2)
                    for h in range(2):
                        dve.wait_ge(*fetched[h].done(2))
                    divide(dve, chain, t["got"], D + 1, t["over"])
                    link(V.tensor_tensor(t["sq"][:], t["got"][:, :, 0:D], wide(t["over"]), ALU.mult))

                    def stage_block(b, r, u):
                        if later(b, 2):
                            dve.wait_ge(*gru["turned"].done(b - 2))
                            dve.wait_ge(*gru["block"].done(b - 2))
                        V.tensor_copy(two[:, u, 0:1, 0:D], X[:, bass.ds(b, 1), :]).then_inc(gru["block"].sem, 1)
                        V.tensor_copy(two[:, u, 1:2, 0:D], t["sq"][:, bass.ds(b, 1), :]).then_inc(gru["block"].sem, 1)

                    def keep(b, r, u):
                        dve.wait_ge(*gru["turned"].done(b))
                        if later(b, 2):
                            dve.wait_ge(*gru["made"].done(b - 2))
                        V.tensor_copy(two_t[:, u].rearrange("p i n -> p (i n)"),
                                      ps[2 + u][:, 0:2 * P]).then_inc(gru["kept"].sem, 1)

                    def reset(b, r, u):
                        dve.wait_ge(*gru["sig"].done(b))
                        if later(b, 2):
                            dve.wait_ge(*gru["tanh"].done(b - 2))
                            dve.wait_ge(*gru["new"].done(b - 2))
                        V.tensor_scalar(gates1[:, u, :], gates[:, u, :], 0.5, 0.5, ALU.mult,
                                        ALU.add).then_inc(gru["part"].sem, 4)
                        dve.wait_ge(*gru["part"].done(b))
                        V.tensor_tensor(cand[:, u, :], gates1[:, u, 0:D], ps[4 + u][:, 3 * D:4 * D],
                                        ALU.mult).then_inc(gru["reset"].sem, 1)
                        dve.wait_ge(*gru["reset"].part(b, 1))
                        V.tensor_tensor(cand[:, u, :], cand[:, u, :], ps[4 + u][:, 2 * D:3 * D],
                                        ALU.add).then_inc(gru["reset"].sem, 1)

                    def update(b, r, u):
                        dve.wait_ge(*gru["tanh"].done(b))
                        nw = gru["new"]
                        V.tensor_tensor(gates[:, u, 0:D], ps[4 + u][:, 4 * D:GW], cand[:, u, :],
                                        ALU.subtract).then_inc(nw.sem, 1)
                        dve.wait_ge(*nw.part(b, 1))
                        V.tensor_tensor(gates[:, u, 0:D], gates[:, u, 0:D], gates1[:, u, D:2 * D],
                                        ALU.mult).then_inc(nw.sem, 1)
                        dve.wait_ge(*nw.part(b, 2))
                        V.tensor_tensor(t["Y"][:, bass.ds(b, 1), :], gates[:, u, None, 0:D], cand[:, u, None, :],
                                        ALU.add).then_inc(nw.sem, 1)

                    steps_of(dve, NB, 2, [(3, update), (1, keep), (0, stage_block), (2, reset)])
                    dve.wait_ge(*gru["new"].done(NB - 1))
                    link(V.tensor_scalar(t["mean"][:], t["got"][:, :, D], 0.0, None, ALU.is_gt))
                    link(V.tensor_copy(own[:], t["mean"][:]))
                    link(V.tensor_copy(t["sq"][:], X[:]))
                    link(V.copy_predicated(t["sq"][:], own[:, :, None].to_broadcast([P, NB, D]), t["Y"][:]))
                    link(V.tensor_tensor(t["Y"][:], t["sq"][:], X[:], ALU.add))
                    norm_vector(dve, chain, 2, t["Y"], (t["sq"], t["mean"], t["var"]))

        far3_turned, far3_kept, near3_made, z3_ready = sem("far3_turned"), sem("far3_kept"), sem("near3_made"), \
            sem("z3_ready")
        w3_loaded = sem("w3_loaded")
        with ExitStack() as ctx:
            Z3 = sbt(ctx, "Z3", [P, NB, D + 1])
            prod = sbt(ctx, "prod", [P, NB, D])
            far3 = sbt(ctx, "far3", [P, NB])
            far3_t = sbt(ctx, "far3_t", [NB, P])
            w3 = sbt(ctx, "w3", [P, 2, D])
            b3 = sbt(ctx, "b3", [P, 1])
            chain = node_chain
            with nc.Block() as block:
                @block.sync
                def _(sp):
                    sp.dma_start(w3[:].rearrange("p e f -> p (e f)"),
                                 A["w3"].to_broadcast([P, 2 * D])).then_inc(w3_loaded, 16)
                    sp.dma_start(b3[:], A["b3"][None, :].to_broadcast([P, 1])).then_inc(w3_loaded, 16)
                    sp.wait_ge(z3_ready, 1)
                    sp.dma_start(table[3].rearrange("(b p) w -> p b w", p=P), Z3[:]).then_inc(stored, 16)
                    sp.wait_ge(stored, 48)

                @block.vector
                def _(dve):
                    link = lambda ins: chain.link(dve, ins)
                    dve.wait_ge(w3_loaded, 32)
                    link(V.tensor_copy(Z3[:, :, 0:D], X[:]))
                    link(V.tensor_tensor(prod[:], X[:], row3(w3[:, 0, :]), ALU.mult))
                    V.tensor_reduce(Z3[:, :, D:D + 1], prod[:], AX, ALU.add).then_inc(z3_ready, 1)
                    dve.wait_ge(z3_ready, 1)
                    link(V.tensor_tensor(prod[:], X[:], row3(w3[:, 1, :]), ALU.mult))
                    link(V.tensor_reduce(far3[:], prod[:], AX, ALU.add))
                    V.tensor_scalar(far3[:], far3[:], b3[:, 0:1], None, ALU.add).then_inc(far3_turned, 1)
                    near_vector(dve, chain, far3_turned, far3_t, far3_kept, near3_made)

                @block.tensor
                def _(pe):
                    near_tensor(pe, far3, far3_turned, far3_t, far3_kept, near3_made)

        edge_layer(3, "d", "plain")
        with ExitStack() as ctx:
            t = node_tiles(ctx, 3, D + 1)
            chain = node_chain
            with nc.Block() as block:
                @block.sync
                def _(sp):
                    fetch(sp, 3, "d", 0, t["got"], D + 1)
                    sp.wait_ge(x_ready, 4)
                    sp.dma_start(out[0:(NB - 1) * P, :].rearrange("(b p) f -> p b f", p=P),
                                 X[:, 0:NB - 1, :]).then_inc(stored, 16)
                    sp.dma_start(out[(NB - 1) * P:, :], X[0:LASTN, NB - 1, :]).then_inc(stored, 16)
                    sp.wait_ge(stored, 16 * 5)

                @block.scalar
                def _(act):
                    fetch(act, 3, "d", 1, t["got"], D + 1)
                    norm_scalar(act, 3, t["var"])

                @block.vector
                def _(dve):
                    link = lambda ins: chain.link(dve, ins)
                    for h in range(2):
                        dve.wait_ge(*fetched[h].done(3))
                    divide(dve, chain, t["got"], D + 1, t["over"])
                    link(V.tensor_tensor(t["Y"][:], t["got"][:, :, 0:D], wide(t["over"]), ALU.mult))
                    link(V.tensor_tensor(t["Y"][:], t["Y"][:], X[:], ALU.add))
                    norm_vector(dve, chain, 3, t["Y"], (t["sq"], t["mean"], t["var"]))


_SHAPES = dict(x="x", src="src", dst="dst", edge_attr_16="e16", edge_attr_2="e2", L0_gnn_W_fc="w_fc",
               L0_gnn_W_attn="w_attn", L0_gnn_W_edge="w_edge", L0_gnn_W_e2n="w_e2n", L0_gnn_W_m1="w_m1",
               L0_gnn_W_m2="w_m2", L2_gnn_W_att1="w_att1", L2_gnn_b_att1="b_att1", L2_gnn_W_att2="w_att2",
               L2_gnn_b_att2="b_att2", L2_gnn_W_lin="w_lin", L2_gnn_b_lin="b_lin", L2_gnn_W_ih="w_ih",
               L2_gnn_b_ih="b_ih", L2_gnn_W_hh="w_hh", L2_gnn_b_hh="b_hh", L3_gnn_W="w3", L3_gnn_b="b3")
_TRANSPOSED = ("w_fc", "w_e2n", "w_att1", "w_lin", "w_ih", "w_hh")


def kernel(**inputs):
    import numpy as np
    import concourse.bacc as bacc
    from concourse.bass_utils import run_bass_kernel_spmd

    nc = bacc.Bacc("TRN2", target_bir_lowering=False, num_devices=1)
    arrays, A = {}, {}

    def give(name, a):
        a = np.ascontiguousarray(a)
        arrays["in_" + name] = a
        A[name] = nc.dram_tensor("in_" + name, a.shape, mybir.dt.from_np(a.dtype), kind="ExternalInput").ap()

    for name, short in _SHAPES.items():
        a = np.asarray(inputs[name])
        give(short, a)
        if short in _TRANSPOSED:
            give(short + "_t", a.T)
    attn = np.asarray(inputs["L0_gnn_W_attn"])
    give("attn_cols", attn[0, :2 * K3 * D].reshape(2 * K3, D).T)
    give("attn_edge", attn[0, 2 * K3 * D:].reshape(E2, 1))
    out = nc.dram_tensor("out", (NODES, D), F32, kind="ExternalOutput").ap()
    build(nc, A, out)
    r = run_bass_kernel_spmd(nc, [arrays], core_ids=[0])
    return r.results[0]["out"]
```
